# Optimizing a Trainium2 kernel written in Bass

```python
import numpy as np
import jax
import jax.numpy as jnp

def _softmax(x, axis=-1):
    return jax.nn.softmax(x, axis=axis)

def _gelu(x):
    return jax.nn.gelu(x, approximate=True)

def _silu(x):
    return jax.nn.silu(x)

def _sigmoid(x):
    return jax.nn.sigmoid(x)

def _layernorm(x, axis=-1, eps=1e-05):
    m = jnp.mean(x, axis=axis, keepdims=True)
    v = jnp.var(x, axis=axis, keepdims=True)
    return (x - m) / jnp.sqrt(v + eps)

def _scatter_add(tgt, idx, src, axis=0):
    return tgt.at[idx].add(src)

def _segment_sum(src, seg, n):
    return jax.ops.segment_sum(src, seg, n)
kernel_name = 'mk_macaron_d1_jaxref_r8_d56d55'

def setup_inputs(seed: int=0):
    np.random.seed(seed)
    _w = jnp.asarray

    def _L0_attn_setup():
        import jax, jax.numpy as jnp
        import numpy as np
        import math
        N_EMBD = 128
        N_HEAD = 16
        BLOCK_SIZE = 128
        B, T = (4, 128)
        key = jax.random.key(seed)
        ks = jax.random.split(key, 7)
        C = N_EMBD
        return {'x': jax.random.normal(ks[0], (B, T, C), dtype=jnp.float32), 'Wqk': jax.random.normal(ks[1], (C, 2 * C), dtype=jnp.float32) * 0.02, 'bqk': jnp.zeros((2 * C,), dtype=jnp.float32), 'Wgate': jax.random.normal(ks[2], (C, N_HEAD), dtype=jnp.float32) * 0.02, 'bgate': jnp.zeros((N_HEAD,), dtype=jnp.float32), 'Wproj': jax.random.normal(ks[3], (C, C), dtype=jnp.float32) * 0.02, 'bproj': jnp.zeros((C,), dtype=jnp.float32)}
    _L0_attn_in = _L0_attn_setup()

    def _L0_ffn_setup():
        import jax, jax.numpy as jnp
        import numpy as np
        B, T, D, E = (4, 128, 128, 8)
        HD = 4 * D
        key = jax.random.key(seed)
        k1, k2, k3, k4 = jax.random.split(key, 4)
        std = 0.5 * D ** (-0.5)
        bound = 3.0 ** 0.5 * std
        x = jax.random.normal(k1, (B, T, D), dtype=jnp.float32)
        router_w = jax.random.normal(k2, (E, D), dtype=jnp.float32) * 0.02
        expert_fc = jax.random.uniform(k3, (E, D, HD), dtype=jnp.float32, minval=-bound, maxval=bound)
        expert_proj = jax.random.normal(k4, (E, D, HD), dtype=jnp.float32) * 0.02
        return {'x': x, 'router_w': router_w, 'expert_fc': expert_fc, 'expert_proj': expert_proj}
    _L0_ffn_in = _L0_ffn_setup()
    _d = {'L0_attn_x': _L0_attn_in['x'], 'L0_attn_Wqk': _L0_attn_in['Wqk'], 'L0_attn_bqk': _L0_attn_in['bqk'], 'L0_attn_Wgate': _L0_attn_in['Wgate'], 'L0_attn_bgate': _L0_attn_in['bgate'], 'L0_attn_Wproj': _L0_attn_in['Wproj'], 'L0_attn_bproj': _L0_attn_in['bproj'], 'L0_ffn_router_w': _L0_ffn_in['router_w'], 'L0_ffn_expert_fc': _L0_ffn_in['expert_fc'], 'L0_ffn_expert_proj': _L0_ffn_in['expert_proj']}
    _x0 = _d['L0_attn_x']
    _d['L0_attn_x'] = jax.random.normal(jax.random.fold_in(jax.random.key(seed), 1), (8, 512, 128), dtype=_x0.dtype)
    del _x0
    return _d

def reference(L0_attn_x, L0_attn_Wqk, L0_attn_bqk, L0_attn_Wgate, L0_attn_bgate, L0_attn_Wproj, L0_attn_bproj, L0_ffn_router_w, L0_ffn_expert_fc, L0_ffn_expert_proj):

    def _L0_attn_ref(x, Wqk, bqk, Wgate, bgate, Wproj, bproj):
        import jax, jax.numpy as jnp
        import numpy as np
        import math
        N_EMBD = 128
        N_HEAD = 16
        BLOCK_SIZE = 128
        B, T = (4, 128)
        Bx, Tx, C = x.shape
        H = N_HEAD
        D = C // H
        windows = jnp.array([max(4, BLOCK_SIZE // 2 ** h) for h in range(H)], dtype=jnp.int32)
        qk = x @ Wqk + bqk
        q, k = jnp.split(qk, 2, axis=-1)
        v = k
        q = q.reshape(Bx, Tx, H, D).transpose(0, 2, 1, 3)
        k = k.reshape(Bx, Tx, H, D).transpose(0, 2, 1, 3)
        v = v.reshape(Bx, Tx, H, D).transpose(0, 2, 1, 3)
        i = jnp.arange(Tx)[:, None]
        j = jnp.arange(Tx)[None, :]
        mask = (j <= i)[None] & (j > i - windows[:, None, None])
        att = jnp.einsum('bhtd,bhsd->bhts', q, k) * (1.0 / math.sqrt(D))
        att = jnp.where(mask[None], att, -jnp.inf)
        att = jax.nn.softmax(att, axis=-1)
        out = jnp.einsum('bhts,bhsd->bhtd', att, v)
        combined = out.transpose(0, 2, 1, 3)
        gates = jax.nn.softmax(x @ Wgate + bgate, axis=-1)
        gated = (combined * gates[..., None]).reshape(Bx, Tx, C)
        return gated @ Wproj + bproj

    def _L0_ffn_ref(x, router_w, expert_fc, expert_proj):
        import jax, jax.numpy as jnp
        import numpy as np
        B, T, D, E = (4, 128, 128, 8)
        HD = 4 * D
        logits = jnp.einsum('btd,ed->bte', x, router_w)
        probs = jax.nn.softmax(logits, axis=-1)
        expert_ids = jnp.argmax(probs, axis=-1)
        mask = jax.nn.one_hot(expert_ids, E, dtype=x.dtype)
        h = jnp.einsum('btd,edh->ebth', x, expert_fc)
        h = jnp.square(jax.nn.relu(h))
        out_e = jnp.einsum('ebth,edh->ebtd', h, expert_proj)
        output = jnp.einsum('ebtd,bte->btd', out_e, mask)
        return output
    x = L0_attn_x
    x = x + 0.5 * _L0_ffn_ref(_layernorm(x, axis=-1), L0_ffn_router_w, L0_ffn_expert_fc, L0_ffn_expert_proj)
    x = x + _L0_attn_ref(_layernorm(x, axis=-1), L0_attn_Wqk, L0_attn_bqk, L0_attn_Wgate, L0_attn_bgate, L0_attn_Wproj, L0_attn_bproj)
    x = x + 0.5 * _L0_ffn_ref(_layernorm(x, axis=-1), L0_ffn_router_w, L0_ffn_expert_fc, L0_ffn_expert_proj)
    return x

_drawn_inputs = setup_inputs


def setup_inputs(seed=0):
    import zlib

    import numpy as np

    out = dict(_drawn_inputs(seed))
    spreads = {'L0_attn_bqk': (0.0, 0.8), 'L0_attn_bgate': (0.0, 0.8), 'L0_attn_bproj': (0.0, 0.1)}
    factors = {'L0_attn_Wqk': 8.0, 'L0_attn_Wgate': 8.0, 'L0_attn_Wproj': 8.0}
    for name, (base, spread) in spreads.items():
        noise = np.random.default_rng([zlib.crc32(name.encode()), seed]).standard_normal(out[name].shape)
        drawn = base * np.exp(spread * noise) if base else spread * noise
        out[name] = jnp.asarray(drawn.astype(out[name].dtype))
    for name, factor in factors.items():
        out[name] = (out[name] * factor).astype(out[name].dtype)
    return out
```

```python
import concourse.bass as bass
from concourse import mybir
from contextlib import ExitStack

B, T, C = 8, 512, 128
N_TILES = B * T // 128
N_HEADS, HEAD = 16, 8
WINDOWS = [max(4, 128 // 2 ** h) for h in range(N_HEADS)]
DENSE = 4
LIGHT = N_HEADS - DENSE
LC = LIGHT * HEAD
SHIFTS = 4
E, HID = 8, 512
KT = HID // 128
HALVES = 2
TH = N_TILES // HALVES
BH = B // HALVES
NBH = TH + E - 1
NB = HALVES * NBH
SCALE = HEAD ** -0.5
EPS = 1e-5
BIG = 1e30
QKG = 2 * C + N_HEADS
PAD = 8

PREV = [min(w, 128) for w in WINDOWS[:DENSE]]
SCORE_AT = []
for h in range(DENSE):
    SCORE_AT.append((h // 2, 0 if h % 2 == 0 else 128 + PREV[h - 1]))
BANK_COLS = [sum(128 + PREV[h] for h in (0, 1)), sum(128 + PREV[h] for h in (2, 3))]

CONST = {"ident": 128, "below": 128, "mask_first": DENSE * 128, "mask_rest": sum(BANK_COLS),
         "light_mask": 4 * LIGHT * 8, "first_of_ties": E, "block_no": NBH, "full_blocks": TH, "head_rows": DENSE}
CONST_AT, _at = {}, 0
for _n, _w in CONST.items():
    CONST_AT[_n] = (_at, _at + _w)
    _at += _w
CONST_COLS = _at


def macaron(nc, x_in, w_qkg, b_qkg, w_q4, w_k4, b_q4, b_k4, w_proj, b_proj, w_router, w_fc, w_out, consts, out):
    f32, bf16, i32, u32 = mybir.dt.float32, mybir.dt.bfloat16, mybir.dt.int32, mybir.dt.uint32
    ALU, ACT, AX = mybir.AluOpType, mybir.ActivationFunctionType, mybir.AxisListType
    ds = bass.ds
    ctx = ExitStack()
    with ctx:
        def sb(name, shape, dt=f32):
            return ctx.enter_context(nc.sbuf_tensor(name, shape, dt))

        def sem(name):
            return ctx.enter_context(nc.semaphore(name))

        bank = [ctx.enter_context(nc.psum_tensor(f"bank{i}", [128, 512], f32)) for i in range(8)]

        x = sb("x", [128, N_TILES, C])
        xn = sb("xn", [128, N_TILES, C])
        yg = sb("yg", [128, N_TILES, C])
        sq = sb("sq", [128, TH, C])
        rowsum = sb("rowsum", [128, N_TILES])
        var = sb("var", [128, N_TILES])
        rstd = sb("rstd", [128, N_TILES])
        newton = sb("newton", [128, TH])
        fc = sb("fc", [128, E, HID])
        wo = sb("wo", [128, E, KT, C])
        wqkg = sb("wqkg", [128, QKG])
        bqkg = sb("bqkg", [128, QKG])
        wq4 = sb("wq4", [128, 128])
        wk4 = sb("wk4", [128, 128])
        bq4 = sb("bq4", [128, DENSE])
        bk4 = sb("bk4", [128, 1])
        wproj = sb("wproj", [128, C])
        bproj = sb("bproj", [128, C])
        wr = sb("wr", [128, E])
        cst = sb("cst", [128, CONST_COLS])
        ones = sb("ones", [128, 128])
        identb = sb("identb", [128, 128], bf16)
        maskb = sb("maskb", [128, DENSE * 128 + sum(BANK_COLS)], bf16)

        def const(name):
            a, b = CONST_AT[name]
            return cst[:, a:b]

        ident = const("ident")
        xnT = sb("xnT", [128, 2, 4 * 128])
        top = sb("top", [128, TH])
        top2 = sb("top2", [128, TH])
        tied = sb("tied", [128, TH, E])
        hot = sb("hot", [128, TH, E])
        cnt = sb("cnt", [128, E, TH])
        upto = sb("upto", [128, E, TH])
        before = sb("before", [128, E, TH])
        n_tok = sb("n_tok", [128, E])
        over = sb("over", [128, E, TH])
        n_blk = sb("n_blk", [128, E])
        blk_end = sb("blk_end", [128, E])
        base = sb("base", [128, E])
        place = sb("place", [128, E, TH])
        slot_e = sb("slot_e", [128, TH, E])
        slot_f = sb("slot_f", [128, TH])
        slot = sb("slot", [128, N_TILES], i32)
        past = sb("past", [1, NBH, E])
        expert_f = sb("expert_f", [1, NBH])
        expert = sb("expert", [1, NB], i32)
        xs = sb("xs", [128, 2, C])
        xT = sb("xT", [128, 2, 128])
        r = sb("r", [128, 2, HID])
        hT = sb("hT", [128, 2, KT, 128])
        ys = sb("ys", [128, 2, C])
        xb = sb("xb", [128, 4, C])
        qT = sb("qT", [128, 2, DENSE, 512])
        kT = sb("kT", [128, 2, 512])
        qkg = sb("qkg", [128, 2, 4, QKG])
        ks = sb("ks", [128, 2, 4, SHIFTS, LC])
        ks4 = sb("ks4", [128, 2, 4, SHIFTS, HEAD])
        prod = sb("prod", [128, 4, SHIFTS, LC])
        prod4 = sb("prod4", [128, 4, SHIFTS, HEAD])
        sc = sb("sc", [128, 4, LIGHT, 8])
        scm = sb("scm", [128, 4, LIGHT, 8])
        lmax = sb("lmax", [128, 4, LIGHT])
        pl = sb("pl", [128, 4, LIGHT, 8])
        osh = sb("osh", [128, 4, LC])
        o4 = sb("o4", [128, 4, HEAD])
        dmax = sb("dmax", [128, 4, DENSE])
        nmax = sb("nmax", [128, 4, DENSE])
        P = sb("P", [128, 2, DENSE, 256])
        PT = sb("PT", [128, 2, DENSE, 2, 128])
        den = sb("den", [128, 4, N_HEADS])
        gmax = sb("gmax", [128, 4])
        gl = sb("gl", [128, 4, N_HEADS])
        ge = sb("ge", [128, 4, N_HEADS])
        gsum = sb("gsum", [128, 4])
        dg = sb("dg", [128, 4, N_HEADS])
        rc = sb("rc", [128, 4, N_HEADS])
        fac = sb("fac", [128, 4, N_HEADS])
        gated = sb("gated", [128, 4, C])
        gT = sb("gT", [128, 512])

        rows_d = nc.dram_tensor("rows_d", [NB * 128, C], f32, kind="Internal")
        y_d = nc.dram_tensor("y_d", [NB * 128, C], f32, kind="Internal")
        k_d = nc.dram_tensor("k_d", [PAD + B * T, LC], f32, kind="Internal")

        x_v = x_in.rearrange("b t c -> (b t) c").rearrange("(n p) c -> p n c", p=128)
        out_v = out.rearrange("b t c -> (b t) c").rearrange("(n p) c -> p n c", p=128)

        x_in_s = [sem(f"x_loaded{h}") for h in range(HALVES)]
        const_s = sem("constants_loaded")
        route_w_s = sem("router_weights_loaded")
        ffn_w_s = sem("expert_weights_loaded")
        att_w_s = sem("attention_weights_loaded")
        cleared_s = sem("buffers_cleared")
        zero_s = sem("dram_padding_zeroed")
        masks_s = sem("masks_cast")
        step_s = sem("vector_step")
        xres_s = sem("residual_updated")
        cent_s = sem("rows_centred")
        sq_s = sem("squares_ready")
        var_s = sem("squares_summed")
        norm_s = sem("rows_normalised")
        rt_px_s = sem("route_rows_transposed")
        rt_xT_s = sem("route_transposes_copied")
        logit_s = sem("logits_ready")
        hot_s = sem("expert_choice_ready")
        rank_s = sem("ranks_ready")
        slot_s = sem("slots_ready")
        scat_s = [sem(f"rows_scattered{h}") for h in range(HALVES)]
        gath_s = [sem(f"outputs_gathered{h}") for h in range(HALVES)]
        ld_s = [sem(f"block_loaded{u}") for u in range(2)]
        st_s = [sem(f"block_stored{u}") for u in range(2)]
        px_s = sem("block_transposed")
        xT_s = sem("block_transpose_copied")
        h_s = sem("hidden_ready")
        r_s = sem("relu_ready")
        rT_s = sem("relu_transposed")
        hT_s = sem("hidden_squared")
        py_s = sem("block_output_ready")
        y_s = sem("block_output_copied")
        bias_s = sem("output_bias_added")
        xb_s = sem("batch_normalised")
        a_px_s = sem("batch_transposed")
        a_xT_s = sem("batch_transpose_copied")
        qk_s = sem("dense_qk_ready")
        qkT_s = sem("dense_qk_copied")
        qkg_p_s = sem("qkg_ready")
        qkg_s = sem("qkg_biased")
        kw_s = sem("keys_written")
        ks_s = [sem(f"shifted_keys_loaded{u}") for u in range(2)]
        s_s = sem("dense_scores_ready")
        nmax_s = sem("dense_max_ready")
        p_s = sem("dense_probs_ready")
        pt_s = sem("dense_probs_transposed")
        ptc_s = sem("dense_probs_copied")
        pv_s = sem("dense_outputs_ready")
        lsc_s = sem("light_scores_ready")
        lp_s = sem("light_probs_ready")
        gl_s = sem("gate_logits_ready")
        ge_s = sem("gates_ready")
        gated_s = sem("gated_ready")
        gp_s = sem("gated_transposed")
        gT_s = sem("gated_copied")
        proj_s = sem("projection_ready")
        att_s = sem("attention_added")
        out_s = sem("output_stored")

        def span(h):
            return slice(h * TH, (h + 1) * TH)

        def shifted(j, u, k):
            q, v = j + (u + k) // 2, (u + k) % 2
            return q, v, q * 2 + v

        block = ctx.enter_context(nc.Block())

        @block.sync
        def _(sp):
            for h in range(HALVES):
                sp.dma_start(x[:, span(h), :], x_v[:, span(h), :]).then_inc(x_in_s[h], 16)
                if h == 0:
                    sp.dma_start(cst[:, :], consts).then_inc(const_s, 16)
                    sp.dma_start(wr[:, :], w_router).then_inc(route_w_s, 16)
            sp.wait_ge(cleared_s, 1)
            for h in range(HALVES):
                sp.dma_start(rows_d[h * NBH * 128:(h + 1) * NBH * 128, :].rearrange("(p n) c -> p n c", p=128),
                             yg[:, 0:NBH, :]).then_inc(zero_s, 16)
            sp.dma_start(k_d[0:PAD, :], yg[0:PAD, 0, 0:LC]).then_inc(zero_s, 16)
            sp.dma_start(fc[:, :, :], w_fc.rearrange("e d h -> d e h")).then_inc(ffn_w_s, 16)
            sp.dma_start(wo[:, :, :, :].rearrange("p e k d -> p (e k) d"),
                         w_out.rearrange("e (k p) d -> p (e k) d", p=128)).then_inc(ffn_w_s, 16)
            for dst, src in ((wqkg, w_qkg), (wq4, w_q4), (wk4, w_k4), (bq4, b_q4), (bk4, b_k4), (wproj, w_proj)):
                sp.dma_start(dst[:, :], src).then_inc(att_w_s, 16)
            sp.dma_start(bqkg[:, :], b_qkg.to_broadcast([128, QKG])).then_inc(att_w_s, 16)
            sp.dma_start(bproj[:, :], b_proj.to_broadcast([128, C])).then_inc(att_w_s, 16)

            def load(f, j, u):
                _, v, b = shifted(j, u, 0)
                sp.dma_start(xs[:, v, :], rows_d[ds(b * 128, 128), :]).then_inc(ld_s[v], 16)

            def store(f, j, u):
                _, v, b = shifted(j, u, 0)
                sp.wait_ge(y_s, b + (NB * f + 1))
                sp.dma_start(y_d[ds(b * 128, 128), :], ys[:, v, :]).then_inc(st_s[v], 16)

            def ffn(f):
                def step(j, u, load_ahead=True, store_back=True, scattered=0):
                    _, _, b = shifted(j, u, 0)
                    if load_ahead:
                        if scattered:
                            sp.wait_ge(scat_s[1], scattered)
                        sp.wait_ge(px_s, b + (NB * f + 1))
                        q, v, _ = shifted(j, u, 2)
                        load(f, q, v)
                    if store_back:
                        q, v, _ = shifted(j, u, -2)
                        store(f, q, v)

                per = 16 * TH
                sp.wait_ge(scat_s[0], per * (f + 1))
                load(f, 0, 0)
                load(f, 0, 1)
                step(0, 0, store_back=False)
                step(0, 1, store_back=False)
                cross = NBH - 2
                with sp.Fori(1, cross // 2) as j:
                    step(j, 0)
                    step(j, 1)
                j = cross // 2
                for u in range(2):
                    step(j, u, scattered=per * (f + 1) if 2 * j + u == cross else 0)
                with sp.Fori(j + 1, NB // 2 - 1) as j:
                    step(j, 0)
                    step(j, 1)
                for u in range(2):
                    step(NB // 2 - 1, u, load_ahead=False)
                store(f, NB // 2 - 1, 0)
                store(f, NB // 2 - 1, 1)

            def keys(i, q, u):
                sp.wait_ge(qkg_s, i * 4 + 4)
                sp.dma_start(k_d[ds(i * T + PAD, T), :].rearrange("(t p) c -> p t c", p=128),
                             qkg[:, u, :, C + DENSE * HEAD:2 * C]).then_inc(kw_s, 16)
                sp.wait_ge(kw_s, i * 16 + 16)
                for s in range(SHIFTS):
                    sp.dma_start(ks[:, u, :, s, :],
                                 k_d[ds(i * T + (PAD + s + 1 - SHIFTS), T), :].rearrange("(t p) c -> p t c", p=128)
                                 ).then_inc(ks_s[u], 16)
                for s in range(SHIFTS):
                    sp.dma_start(ks4[:, u, :, s, :],
                                 k_d[ds(i * T + (PAD + s + 1 - 2 * SHIFTS), T), 0:HEAD].rearrange(
                                     "(t p) c -> p t c", p=128)).then_inc(ks_s[u], 16)

            ffn(0)
            sp.wait_ge(zero_s, 48)
            for i in range(B):
                keys(i, i // 2, i % 2)
            ffn(1)
            for h in range(HALVES):
                sp.wait_ge(xres_s, HALVES + h + 1)
                sp.dma_start(out_v[:, span(h), :], x[:, span(h), :]).then_inc(out_s, 16)
            sp.wait_ge(out_s, 16 * HALVES)

        @block.gpsimd
        def _(pool):
            pool.memset(yg[:, 0:NBH, :], 0.0).then_inc(cleared_s, 1)
            pool.memset(ones[:, :], 1.0).then_inc(cleared_s, 1)
            pool.memset(P[:, :, :, :], 0.0).then_inc(cleared_s, 1)
            pool.memset(sc[:, :, :, :], 0.0).then_inc(cleared_s, 1)

            def scatter(f, h):
                pool.wait_ge(slot_s, HALVES * f + h + 1)
                for t in range(h * TH, (h + 1) * TH):
                    pool.indirect_dma_start(
                        out=rows_d[:, :], out_offset=bass.IndirectOffsetOnAxis(ap=slot[:, t:t + 1].bitcast(u32), axis=0),
                        in_=xn[:, t, :], in_offset=None).then_inc(scat_s[h], 16)

            def gather(f, h):
                for u in range(2):
                    blocks = len([b for b in range((h + 1) * NBH) if b % 2 == u])
                    pool.wait_ge(st_s[u], 16 * (NB // 2 * f + blocks))
                for t in range(h * TH, (h + 1) * TH):
                    pool.indirect_dma_start(
                        out=yg[:, t, :], out_offset=None, in_=y_d[0:(h + 1) * NBH * 128, :],
                        in_offset=bass.IndirectOffsetOnAxis(ap=slot[:, t:t + 1].bitcast(u32), axis=0)
                    ).then_inc(gath_s[h], 16)

            def squares(h):
                pool.wait_ge(cent_s, HALVES + h + 1)
                pool.tensor_tensor(sq[:, :, :], xn[:, span(h), :], xn[:, span(h), :], ALU.mult).then_inc(sq_s, 1)
                pool.wait_ge(att_w_s, 16 * 8)
                pool.tensor_tensor(x[:, span(h), :], x[:, span(h), :],
                                   bproj[:, :].unsqueeze(1).to_broadcast([128, TH, C]), ALU.add).then_inc(bias_s, 1)

            pool.wait_ge(zero_s, 48)
            scatter(0, 0)
            scatter(0, 1)
            gather(0, 0)
            squares(0)
            gather(0, 1)
            squares(1)
            scatter(1, 0)
            scatter(1, 1)
            gather(1, 0)
            gather(1, 1)

        @block.scalar
        def _(act):
            act.preload_act_table(ACT.Exp)
            act.wait_ge(const_s, 16)
            act.activation(identb[:, :], ident, ACT.Copy).then_inc(masks_s, 1)
            a, b_ = CONST_AT["mask_first"][0], CONST_AT["mask_rest"][1]
            act.activation(maskb[:, :], cst[:, a:b_], ACT.Copy).then_inc(masks_s, 1)

            def squares(n, h):
                act.wait_ge(cent_s, n + 1)
                if n:
                    act.wait_ge(var_s, n)
                act.activation(sq[:, :, :], xn[:, span(h), :], ACT.Square).then_inc(sq_s, 1)

            def route(f, h):
                for g in range(BH):
                    n = (HALVES * f + h) * BH + g
                    act.wait_ge(rt_px_s, n + 1)
                    if n >= 2:
                        act.wait_ge(logit_s, n - 1)
                    act.activation(xnT[:, n % 2, :], bank[6][:, :], ACT.Copy).then_inc(rt_xT_s, 1)

            def ffn_step(f, j, u, first=True, mid=True, last=True):
                _, _, b = shifted(j, u, 0)
                n = b + NB * f
                if first:
                    q, v, _ = shifted(j, u, 1)
                    act.wait_ge(px_s, n + 2)
                    if mid:
                        act.wait_ge(h_s, n)
                    act.activation(xT[:, v, :], bank[5][:, 0:128], ACT.Copy).then_inc(xT_s, 1)
                if mid:
                    q, v, _ = shifted(j, u, -1)
                    act.wait_ge(rT_s, n)
                    if last == 1:
                        act.wait_ge(py_s, n - 2)
                    act.activation(hT[:, v, :, :], bank[2 + v][:, :].rearrange("p (k c) -> p k c", k=KT),
                                   ACT.Square).then_inc(hT_s, 1)
                if last:
                    q, v, _ = shifted(j, u, -2)
                    act.wait_ge(py_s, n - 1)
                    if last == 1:
                        act.wait_ge(st_s[v], (q + NB // 2 * f) * 16)
                    act.activation(ys[:, v, :], bank[4][:, 0:128], ACT.Copy).then_inc(y_s, 1)

            def ffn(f, mid_at=None, mid_work=None):
                act.wait_ge(px_s, NB * f + 1)
                act.activation(xT[:, 0, :], bank[5][:, 0:128], ACT.Copy).then_inc(xT_s, 1)
                ffn_step(f, 0, 0, mid=False, last=0)
                ffn_step(f, 0, 1, last=0)
                ffn_step(f, 1, 0, last=2)
                ffn_step(f, 1, 1, last=1)
                lo = 2
                if mid_work:
                    with act.Fori(lo, mid_at) as j:
                        ffn_step(f, j, 0)
                        ffn_step(f, j, 1)
                    mid_work()
                    lo = mid_at
                with act.Fori(lo, NB // 2 - 1) as j:
                    ffn_step(f, j, 0)
                    ffn_step(f, j, 1)
                ffn_step(f, NB // 2 - 1, 0)
                ffn_step(f, NB // 2 - 1, 1, first=False)
                ffn_step(f, NB // 2, 0, first=False)
                ffn_step(f, NB // 2, 1, first=False, mid=False)

            def project(i, u, first):
                act.wait_ge(a_px_s, i + 1)
                if not first:
                    act.wait_ge(qkg_p_s, i * 4 - 4)
                act.activation(xnT[:, u, :], bank[5][:, :], ACT.Copy).then_inc(a_xT_s, 1)
                act.wait_ge(qk_s, i * 2 + 1)
                for h in range(DENSE):
                    act.activation(qT[:, u, h, :], bank[6][:, :], ACT.Identity, bias=bq4[:, h:h + 1],
                                   scale=const("head_rows")[:, h:h + 1]).then_inc(qkT_s, 1)
                act.wait_ge(qk_s, i * 2 + 2)
                act.activation(kT[:, u, :], bank[7][:, :], ACT.Identity, bias=bk4[:, 0:1]).then_inc(qkT_s, 1)

            def dense_probs(i, t):
                act.wait_ge(nmax_s, i * 4 + (t + 1))
                for h in range(DENSE):
                    if t == 0:
                        s, p = bank[0][:, h * 128:(h + 1) * 128], P[:, 0, h, 128:256]
                    else:
                        k, a0 = SCORE_AT[h]
                        w = 128 + PREV[h]
                        s, p = bank[k][:, a0:a0 + w], P[:, t % 2, h, 256 - w:256]
                    act.activation(p, s, ACT.Exp, bias=nmax[:, t, h:h + 1], scale=SCALE,
                                   accum_out=den[:, t, h:h + 1]).then_inc(p_s, 1)

            def copy_probs(i, t):
                for k in range(1 if t == 0 else 2):
                    act.wait_ge(pt_s, i * 7 + ((1 if t == 0 else 2 * t) + k))
                    if t == 0:
                        dst = PT[:, 0, :, 1, :]
                        src = bank[2][:, :].rearrange("p (h q) -> p h q", h=DENSE)
                    else:
                        dst = PT[:, t % 2, 2 * k:2 * k + 2, :, :].rearrange("p h a q -> p (h a q)")
                        src = bank[2 + k][:, :]
                    act.activation(dst, src, ACT.Copy).then_inc(ptc_s, 1)

            def attend(i, u, ahead):
                act.wait_ge(gl_s, i + 1)
                act.activation(ge[:, :, :], gl[:, :, :], ACT.Exp).then_inc(ge_s, 1)
                dense_probs(i, 0)
                copy_probs(i, 0)
                dense_probs(i, 1)
                act.wait_ge(lsc_s, i + 1)
                act.activation(pl[:, :, :, :], scm[:, :, :, :], ACT.Exp, scale=SCALE).then_inc(lp_s, 1)
                copy_probs(i, 1)
                dense_probs(i, 2)
                if ahead:
                    project(i + 1, 1 - u, False)
                copy_probs(i, 2)
                dense_probs(i, 3)
                copy_probs(i, 3)
                act.wait_ge(gp_s, i + 1)
                act.activation(gT[:, :], bank[6][:, :], ACT.Copy).then_inc(gT_s, 1)

            squares(0, 0)
            route(0, 0)
            squares(1, 1)
            route(0, 1)
            ffn(0)
            act.wait_ge(att_w_s, 16 * 8)
            project(0, 0, True)
            for i in range(B):
                attend(i, i % 2, i + 1 < B)
                if i == BH - 1:
                    squares(4, 0)
                if i == BH + 1:
                    route(1, 0)
            ffn(1, 4, lambda: (squares(5, 1), route(1, 1)))

        @block.vector
        def _(dve):
            steps = [0]

            def step(ins):
                steps[0] += 1
                ins.then_inc(step_s, 1)
                dve.wait_ge(step_s, steps[0])

            def centre(n, h):
                step(nc.vector.tensor_reduce(rowsum[:, span(h)], x[:, span(h), :], AX.X, ALU.add))
                nc.vector.scalar_tensor_tensor(
                    xn[:, span(h), :], rowsum[:, span(h)].unsqueeze(2).to_broadcast([128, TH, C]), -1.0 / C,
                    x[:, span(h), :], ALU.mult, ALU.add).then_inc(cent_s, 1)

            def spread(n, h):
                dve.wait_ge(sq_s, n + 1)
                nc.vector.tensor_reduce(var[:, span(h)], sq[:, :, :], AX.X, ALU.add).then_inc(var_s, 1)
                dve.wait_ge(var_s, n + 1)
                step(nc.vector.tensor_scalar(var[:, span(h)], var[:, span(h)], 1.0 / C, EPS, ALU.mult, ALU.add))
                step(nc.vector.tensor_scalar(rstd[:, span(h)].bitcast(i32), var[:, span(h)].bitcast(i32),
                                             -0.5, float(0x5f3759df), ALU.mult, ALU.add))
                for _ in range(3):
                    step(nc.vector.tensor_tensor(newton[:, :], rstd[:, span(h)], rstd[:, span(h)], ALU.mult))
                    step(nc.vector.scalar_tensor_tensor(newton[:, :], newton[:, :], -0.5, var[:, span(h)],
                                                        ALU.mult, ALU.mult))
                    step(nc.vector.scalar_tensor_tensor(rstd[:, span(h)], newton[:, :], 1.5, rstd[:, span(h)],
                                                        ALU.add, ALU.mult))

            def normalise(h):
                nc.vector.tensor_tensor(xn[:, span(h), :], xn[:, span(h), :],
                                        rstd[:, span(h)].unsqueeze(2).to_broadcast([128, TH, C]),
                                        ALU.mult).then_inc(norm_s, 1)

            def route(f, h):
                n = HALVES * f + h
                logits = bank[7][:, 0:TH * E].rearrange("p (t e) -> p t e", e=E)
                ranks = bank[7][:, 128:128 + TH * E].rearrange("p (t e) -> p t e", e=E)
                counts = bank[7][:, 256:256 + TH * E].rearrange("p (t e) -> p e t", e=E)

                def along(ap):
                    return ap.unsqueeze(2).to_broadcast([128, TH, E])

                dve.wait_ge(logit_s, BH * (n + 1))
                step(nc.vector.tensor_reduce(top[:, :], logits, AX.X, ALU.max))
                step(nc.vector.tensor_tensor(tied[:, :, :], logits, along(top[:, :]), ALU.is_equal))
                step(nc.vector.tensor_tensor(tied[:, :, :], tied[:, :, :],
                                             const("first_of_ties").unsqueeze(1).to_broadcast([128, TH, E]), ALU.mult))
                step(nc.vector.tensor_reduce(top2[:, :], tied[:, :, :], AX.X, ALU.max))
                nc.vector.tensor_tensor(hot[:, :, :], tied[:, :, :], along(top2[:, :]),
                                        ALU.is_equal).then_inc(hot_s, 1)
                dve.wait_ge(rank_s, n + 1)
                step(nc.vector.tensor_copy(cnt[:, :, :], counts))
                flat = lambda a: a[:, :, :].rearrange("p e t -> p (e t)")
                step(nc.vector.tensor_tensor_scan(flat(upto), ones[:, :], flat(cnt), 0.0, ALU.mult, ALU.add))
                step(nc.vector.tensor_tensor(before[:, :, :], upto[:, :, :], cnt[:, :, :], ALU.subtract))
                step(nc.vector.tensor_tensor(n_tok[:, :], upto[:, :, TH - 1], before[:, :, 0], ALU.subtract))
                step(nc.vector.tensor_tensor(over[:, :, :], n_tok[:, :].unsqueeze(2).to_broadcast([128, E, TH]),
                                             const("full_blocks").unsqueeze(1).to_broadcast([128, E, TH]), ALU.is_gt))
                step(nc.vector.tensor_reduce(n_blk[:, :], over[:, :, :], AX.X, ALU.add))
                step(nc.vector.tensor_tensor_scan(blk_end[:, :], ones[:, 0:E], n_blk[:, :], 0.0, ALU.mult, ALU.add))
                step(nc.vector.tensor_tensor(base[:, :], blk_end[:, :], n_blk[:, :], ALU.subtract))
                step(nc.vector.scalar_tensor_tensor(base[:, :], base[:, :], 128.0, before[:, :, 0],
                                                    ALU.mult, ALU.subtract))
                step(nc.vector.tensor_tensor(past[:, :, :], const("block_no")[0:1, :].unsqueeze(2).to_broadcast([1, NBH, E]),
                                             blk_end[0:1, :].unsqueeze(1).to_broadcast([1, NBH, E]), ALU.is_ge))
                step(nc.vector.tensor_reduce(expert_f[:, :], past[:, :, :], AX.X, ALU.add))
                step(nc.vector.tensor_scalar(expert[:, h * NBH:(h + 1) * NBH], expert_f[:, :], float(E - 1), None, ALU.min))
                step(nc.vector.tensor_tensor(place[:, :, :], before[:, :, :],
                                             base[:, :].unsqueeze(2).to_broadcast([128, E, TH]), ALU.add))
                step(nc.vector.tensor_tensor(slot_e[:, :, :], place[:, :, :].rearrange("p e t -> p t e"), ranks, ALU.add))
                step(nc.vector.tensor_tensor(slot_e[:, :, :], slot_e[:, :, :], hot[:, :, :], ALU.mult))
                step(nc.vector.tensor_reduce(slot_f[:, :], slot_e[:, :, :], AX.X, ALU.add))
                nc.vector.tensor_scalar(slot[:, span(h)], slot_f[:, :], float(h * NBH * 128), None,
                                        ALU.add).then_inc(slot_s, 1)

            def relu(f, j, u, settled=True):
                _, v, b = shifted(j, u, 0)
                n = b + NB * f
                dve.wait_ge(h_s, n + 1)
                if settled:
                    dve.wait_ge(rT_s, n - 1)
                nc.vector.tensor_scalar(r[:, v, :], bank[v][:, :], 0.0, None, ALU.max).then_inc(r_s, 1)

            def half_residual(f, h):
                dve.wait_ge(gath_s[h], 16 * TH * (f + 1))
                nc.vector.scalar_tensor_tensor(x[:, span(h), :], yg[:, span(h), :], 0.5, x[:, span(h), :],
                                               ALU.mult, ALU.add).then_inc(xres_s, 1)
                dve.wait_ge(xres_s, HALVES * f + h + 1)

            def ffn(f, mid_at=None, mid_work=None):
                relu(f, 0, 0, False)
                relu(f, 0, 1, False)
                lo = 1
                if mid_work:
                    with dve.Fori(lo, mid_at) as j:
                        relu(f, j, 0)
                        relu(f, j, 1)
                    mid_work()
                    lo = mid_at
                with dve.Fori(lo, NB // 2) as j:
                    relu(f, j, 0)
                    relu(f, j, 1)

            def normalise_batch(i, first):
                if not first:
                    dve.wait_ge(a_px_s, i)
                nc.vector.tensor_tensor(xb[:, :, :], xn[:, ds(i * 4, 4), :],
                                        rstd[:, ds(i * 4, 4)].unsqueeze(2).to_broadcast([128, 4, C]),
                                        ALU.mult).then_inc(xb_s, 1)

            def add_bias(i, u, t):
                dve.wait_ge(qkg_p_s, i * 4 + (t + 1))
                nc.vector.tensor_tensor(qkg[:, u, t, :], bank[5 + t % 3][:, 0:QKG], bqkg[:, :],
                                        ALU.add).then_inc(qkg_s, 1)

            def dense_max(i, t):
                dve.wait_ge(s_s, i * 4 + (t + 1))
                if t == 0:
                    step(nc.vector.tensor_reduce(dmax[:, t, :], bank[0][:, :].rearrange("p (h k) -> p h k", h=DENSE),
                                                 AX.X, ALU.max))
                else:
                    for h in range(DENSE):
                        k, a0 = SCORE_AT[h]
                        step(nc.vector.tensor_reduce(dmax[:, t, h:h + 1], bank[k][:, a0:a0 + 128 + PREV[h]],
                                                     AX.X, ALU.max))
                nc.vector.tensor_scalar(nmax[:, t, :], dmax[:, t, :], -SCALE, None, ALU.mult).then_inc(nmax_s, 1)

            def over_d(a):
                return a.unsqueeze(a.ndim).to_broadcast(list(a.shape) + [HEAD])

            def light_scores(i, q, u):
                lq = qkg[:, u, :, DENSE * HEAD:C]
                dve.wait_ge(ks_s[u], q * (32 * SHIFTS) + 32 * SHIFTS)
                nc.vector.tensor_tensor(prod[:, :, :, :], ks[:, u, :, :, :],
                                        lq.unsqueeze(2).to_broadcast([128, 4, SHIFTS, LC]), ALU.mult).then_inc(step_s, 1)
                step(nc.vector.tensor_tensor(prod4[:, :, :, :], ks4[:, u, :, :, :],
                                             lq[:, :, 0:HEAD].unsqueeze(2).to_broadcast([128, 4, SHIFTS, HEAD]), ALU.mult))
                steps[0] += 1
                dve.wait_ge(step_s, steps[0])
                for t in range(4):
                    nc.vector.tensor_reduce(
                        sc[:, t, :, SHIFTS:].rearrange("p h s -> p s h"),
                        prod[:, t, :, :].rearrange("p s (h d) -> p s h d", d=HEAD), AX.X, ALU.add).then_inc(step_s, 1)
                steps[0] += 4
                step(nc.vector.tensor_reduce(sc[:, :, 0, 0:SHIFTS], prod4[:, :, :, :], AX.X, ALU.add))
                step(nc.vector.tensor_tensor(scm[:, :, :, :], sc[:, :, :, :],
                                             const("light_mask").rearrange("p (t h s) -> p t h s", t=4, h=LIGHT), ALU.add))
                step(nc.vector.tensor_reduce(lmax[:, :, :], scm[:, :, :, :], AX.X, ALU.max))
                nc.vector.tensor_tensor(scm[:, :, :, :].rearrange("p t h s -> p (t h) s"),
                                        scm[:, :, :, :].rearrange("p t h s -> p (t h) s"),
                                        lmax[:, :, :].rearrange("p t h -> p (t h)").unsqueeze(2).to_broadcast([128, 4 * LIGHT, 8]),
                                        ALU.subtract).then_inc(lsc_s, 1)

            def gate_logits(i, u):
                g = qkg[:, u, :, 2 * C:]
                dve.wait_ge(qkg_s, i * 4 + 4)
                step(nc.vector.tensor_reduce(gmax[:, :], g, AX.X, ALU.max))
                nc.vector.tensor_tensor(gl[:, :, :], g, gmax[:, :].unsqueeze(2).to_broadcast([128, 4, N_HEADS]),
                                        ALU.subtract).then_inc(gl_s, 1)

            def light_outputs(i, u):
                dve.wait_ge(lp_s, i + 1)
                nc.vector.tensor_reduce(den[:, :, DENSE:], pl[:, :, :, :], AX.X, ALU.add).then_inc(step_s, 1)
                steps[0] += 1
                for s in range(SHIFTS):
                    nc.vector.tensor_tensor(prod[:, :, s, :].rearrange("p t (h d) -> p t h d", d=HEAD),
                                            ks[:, u, :, s, :].rearrange("p t (h d) -> p t h d", d=HEAD),
                                            over_d(pl[:, :, :, SHIFTS + s]), ALU.mult).then_inc(step_s, 1)
                steps[0] += SHIFTS
                step(nc.vector.tensor_tensor(prod4[:, :, :, :], ks4[:, u, :, :, :], over_d(pl[:, :, 0, 0:SHIFTS]), ALU.mult))
                nc.vector.tensor_reduce(osh[:, :, :], prod[:, :, :, :].rearrange("p t s c -> p t c s"), AX.X,
                                        ALU.add).then_inc(step_s, 1)
                steps[0] += 1
                step(nc.vector.tensor_reduce(o4[:, :, :], prod4[:, :, :, :].rearrange("p t s d -> p t d s"), AX.X, ALU.add))
                step(nc.vector.tensor_tensor(osh[:, :, 0:HEAD], osh[:, :, 0:HEAD], o4[:, :, :], ALU.add))

            def gate(i, u):
                dve.wait_ge(ge_s, i + 1)
                step(nc.vector.tensor_reduce(gsum[:, :], ge[:, :, :], AX.X, ALU.add))
                dve.wait_ge(p_s, i * 16 + 16)
                step(nc.vector.tensor_tensor(dg[:, :, :], den[:, :, :], gsum[:, :].unsqueeze(2).to_broadcast([128, 4, N_HEADS]),
                                             ALU.mult))
                step(nc.vector.reciprocal(rc[:, :, :], dg[:, :, :]))
                step(nc.vector.tensor_tensor(fac[:, :, :], ge[:, :, :], rc[:, :, :], ALU.mult))
                step(nc.vector.tensor_tensor(gated[:, :, DENSE * HEAD:].rearrange("p t (h d) -> p t h d", d=HEAD),
                                             osh[:, :, :].rearrange("p t (h d) -> p t h d", d=HEAD),
                                             over_d(fac[:, :, DENSE:]), ALU.mult))
                dve.wait_ge(pv_s, i * 4 + 4)
                nc.vector.tensor_tensor(gated[:, :, 0:DENSE * HEAD].rearrange("p t (h d) -> p t h d", d=HEAD),
                                        bank[4][:, 0:4 * DENSE * HEAD].rearrange("p (t h d) -> p t h d", t=4, d=HEAD),
                                        over_d(fac[:, :, 0:DENSE]), ALU.mult).then_inc(gated_s, 1)

            def attended(i, h):
                dve.wait_ge(proj_s, i + 1)
                dve.wait_ge(bias_s, h + 1)
                nc.vector.tensor_tensor(x[:, ds(i * 4, 4), :], bank[7][:, :].rearrange("p (t c) -> p t c", t=4),
                                        x[:, ds(i * 4, 4), :], ALU.add).then_inc(att_s, 1)

            def attend(i, q, u, ahead, h):
                gate_logits(i, u)
                dense_max(i, 0)
                dense_max(i, 1)
                light_scores(i, q, u)
                if ahead:
                    normalise_batch(i + 1, False)
                dense_max(i, 2)
                light_outputs(i, u)
                dense_max(i, 3)
                if ahead:
                    for t in range(4):
                        add_bias(i + 1, 1 - u, t)
                gate(i, u)
                attended(i, h)

            dve.wait_ge(const_s, 16)
            dve.wait_ge(cleared_s, 4)
            for h in range(HALVES):
                dve.wait_ge(x_in_s[h], 16)
                centre(h, h)
                spread(h, h)
                normalise(h)
                if h == 0:
                    pass
                route(0, h)
            ffn(0)
            dve.wait_ge(att_w_s, 16 * 8)
            for h in range(HALVES):
                half_residual(0, h)
                centre(2 + h, h)
                spread(2 + h, h)
            normalise_batch(0, True)
            for t in range(4):
                add_bias(0, 0, t)
            for i in range(B):
                attend(i, i // 2, i % 2, i + 1 < B, i // BH)
                if i == BH - 1:
                    dve.wait_ge(att_s, BH)
                    centre(4, 0)
                    spread(4, 0)
                    normalise(0)
                if i == BH + 1:
                    route(1, 0)
            dve.wait_ge(att_s, B)
            centre(5, 1)

            def second_route():
                spread(5, 1)
                normalise(1)
                route(1, 1)

            ffn(1, 4, second_route)
            for h in range(HALVES):
                half_residual(1, h)

        @block.tensor
        def _(pe):
            def route(f, h):
                n = HALVES * f + h
                pe.wait_ge(norm_s, n + 1)
                for g in range(BH):
                    m = n * BH + g
                    if m:
                        pe.wait_ge(rt_xT_s, m)
                    for t in range(4):
                        mm = pe.transpose(bank[6][:, t * 128:(t + 1) * 128], xn[:, h * TH + g * 4 + t, :], ident)
                    mm.then_inc(rt_px_s, 1)
                    pe.wait_ge(rt_xT_s, m + 1)
                    for t in range(4):
                        a = (g * 4 + t) * E
                        mm = pe.matmul(bank[7][:, a:a + E], xnT[:, m % 2, t * 128:(t + 1) * 128], wr[:, :],
                                       start=True, stop=True)
                    mm.then_inc(logit_s, 1)

            def rank(f, h):
                n = HALVES * f + h
                pe.wait_ge(hot_s, n + 1)
                choice = hot[:, :, :].rearrange("p t e -> p (t e)")
                pe.matmul(bank[7][:, 128:256], const("below"), choice, start=True, stop=True)
                pe.matmul(bank[7][:, 256:384], ones[:, :], choice, start=True, stop=True).then_inc(rank_s, 1)

            def ffn_step(f, j, u, ahead=True, mid=True, r_back=1, y_back=1):
                _, v, b = shifted(j, u, 0)
                n = b + NB * f
                if mid:
                    e = pe.value_load(expert[0:1, ds(b, 1)], min_val=0, max_val=E - 1)
                if ahead:
                    q, w, _ = shifted(j, u, 1)
                    pe.wait_ge(ld_s[w], (q + (NB // 2 * f + 1)) * 16)
                    pe.wait_ge(xT_s, n + 1)
                    pe.transpose(bank[5][:, 0:128], xs[:, w, :], ident).then_inc(px_s, 1)
                if mid:
                    pe.wait_ge(xT_s, n + 1)
                    if r_back == 1 and y_back != 3:
                        pe.wait_ge(r_s, n - 1)
                    pe.matmul(bank[v][:, :], xT[:, v, :], fc[:, ds(e, 1), :], start=True, stop=True).then_inc(h_s, 1)
                    experts[v] = e
                if r_back:
                    _, w, _ = shifted(j, u, -1)
                    pe.wait_ge(r_s, n)
                    if y_back == 1:
                        pe.wait_ge(hT_s, n - 2)
                    for k in range(KT):
                        mm = pe.transpose(bank[2 + w][:, k * 128:(k + 1) * 128], r[:, w, k * 128:(k + 1) * 128], ident)
                    mm.then_inc(rT_s, 1)
                if y_back in (1, 2):
                    _, w, b2 = shifted(j, u, -2)
                    e2 = pe.value_load(expert[0:1, ds(b2, 1)], min_val=0, max_val=E - 1)
                    pe.wait_ge(hT_s, n - 1)
                    if y_back == 1:
                        pe.wait_ge(y_s, n - 2)
                    for k in range(KT):
                        mm = pe.matmul(bank[4][:, 0:128], hT[:, w, k, :], wo[:, ds(e2, 1), k, :],
                                       start=(k == 0), stop=(k == KT - 1))
                    mm.then_inc(py_s, 1)

            experts = [None, None]

            def ffn(f, mid_at=None, mid_work=None):
                pe.wait_ge(ffn_w_s, 32)
                pe.wait_ge(ld_s[0], (NB // 2 * f + 1) * 16)
                pe.transpose(bank[5][:, 0:128], xs[:, 0, :], ident).then_inc(px_s, 1)
                ffn_step(f, 0, 0, r_back=0, y_back=0)
                ffn_step(f, 0, 1, y_back=3)
                ffn_step(f, 1, 0, y_back=2)
                ffn_step(f, 1, 1)
                lo = 2
                if mid_work:
                    with pe.Fori(lo, mid_at) as j:
                        ffn_step(f, j, 0)
                        ffn_step(f, j, 1)
                    mid_work()
                    lo = mid_at
                with pe.Fori(lo, NB // 2 - 1) as j:
                    ffn_step(f, j, 0)
                    ffn_step(f, j, 1)
                ffn_step(f, NB // 2 - 1, 0)
                ffn_step(f, NB // 2 - 1, 1, ahead=False)
                ffn_step(f, NB // 2, 0, ahead=False, mid=False)
                ffn_step(f, NB // 2, 1, ahead=False, mid=False, r_back=0)

            def transpose_batch(i):
                pe.wait_ge(xb_s, i + 1)
                for t in range(4):
                    mm = pe.transpose(bank[5][:, t * 128:(t + 1) * 128], xb[:, t, :], ident)
                mm.then_inc(a_px_s, 1)

            def project_dense(i, u):
                pe.wait_ge(a_xT_s, i + 1)
                if i >= 2:
                    pe.wait_ge(att_s, i - 1)
                for k, w in enumerate((wq4, wk4)):
                    pe.matmul(bank[6 + k][:, :], w[:, :], xnT[:, u, :], start=True, stop=True).then_inc(qk_s, 1)

            def project_tile(i, u, t):
                if t == 1:
                    pe.wait_ge(qkT_s, i * (DENSE + 1) + DENSE)
                if t == 2:
                    pe.wait_ge(qkT_s, i * (DENSE + 1) + DENSE + 1)
                if t == 3:
                    pe.wait_ge(qkg_s, i * 4 + 1)
                pe.matmul(bank[5 + t % 3][:, 0:QKG], xnT[:, u, t * 128:(t + 1) * 128], wqkg[:, :],
                          start=True, stop=True).then_inc(qkg_p_s, 1)

            def scores(i, u, t, first):
                if t == 0:
                    pe.wait_ge(qkT_s, i * (DENSE + 1) + DENSE + 1)
                if not (first and t == 0):
                    pe.wait_ge(p_s, i * 16 + t * 4)
                if t == 0:
                    pe.matmul(bank[0][:, :], identb[:, :], maskb[:, 0:DENSE * 128], start=True, stop=False)
                else:
                    a = DENSE * 128
                    for k in range(2):
                        pe.matmul(bank[k][:, 0:BANK_COLS[k]], identb[:, :], maskb[:, a:a + BANK_COLS[k]],
                                  start=True, stop=False)
                        a += BANK_COLS[k]
                for h in range(DENSE):
                    if t == 0:
                        k, a0, w = 0, h * 128, 128
                        last = h == DENSE - 1
                    else:
                        (k, a0), w = SCORE_AT[h], 128 + PREV[h]
                        last = h % 2 == 1
                    mm = pe.matmul(bank[k][:, a0:a0 + w], qT[:, u, h, t * 128:(t + 1) * 128],
                                   kT[:, u, (t + 1) * 128 - w:(t + 1) * 128], start=False, stop=last)
                mm.then_inc(s_s, 1)

            def turn_probs(i, t, first):
                for k in range(1 if t == 0 else 2):
                    pe.wait_ge(p_s, i * 16 + (t * 4 + (4 if t == 0 else 2 * k + 2)))
                    if t:
                        pe.wait_ge(ptc_s, i * 7 + (1 if t == 1 else 2 * t - 2 + k))
                    for c in range(4):
                        if t == 0:
                            src = P[:, 0, c, 128:256]
                        else:
                            src = P[:, t % 2, 2 * k + c // 2, 128 * (c % 2):128 * (c % 2) + 128]
                        mm = pe.transpose(bank[2 + k][:, c * 128:(c + 1) * 128], src, ident)
                    mm.then_inc(pt_s, 1)

            def outputs(i, u, t):
                v0 = C
                pe.wait_ge(ptc_s, i * 7 + (2 * t + 1))
                for h in range(DENSE):
                    o = bank[4][:, t * DENSE * HEAD + h * HEAD:t * DENSE * HEAD + (h + 1) * HEAD]
                    v = slice(v0 + h * HEAD, v0 + (h + 1) * HEAD)
                    mm = pe.matmul(o, PT[:, t % 2, h, 1, :], qkg[:, u, t, v], start=True, stop=(t == 0))
                    if t:
                        mm = pe.matmul(o, PT[:, t % 2, h, 0, :], qkg[:, u, t - 1, v], start=False, stop=True)
                mm.then_inc(pv_s, 1)

            def finish(i):
                pe.wait_ge(gated_s, i + 1)
                for t in range(4):
                    mm = pe.transpose(bank[6][:, t * 128:(t + 1) * 128], gated[:, t, :], ident)
                mm.then_inc(gp_s, 1)
                pe.wait_ge(gT_s, i + 1)
                for t in range(4):
                    mm = pe.matmul(bank[7][:, t * 128:(t + 1) * 128], gT[:, t * 128:(t + 1) * 128], wproj[:, :],
                                   start=True, stop=True)
                mm.then_inc(proj_s, 1)

            def attend(i, u, ahead, first):
                pe.wait_ge(qkg_s, i * 4 + 4)
                scores(i, u, 0, first)
                turn_probs(i, 0, first)
                scores(i, u, 1, first)
                outputs(i, u, 0)
                turn_probs(i, 1, first)
                scores(i, u, 2, first)
                if ahead:
                    transpose_batch(i + 1)
                outputs(i, u, 1)
                turn_probs(i, 2, first)
                if ahead:
                    project_dense(i + 1, 1 - u)
                scores(i, u, 3, first)
                outputs(i, u, 2)
                turn_probs(i, 3, first)
                if ahead:
                    for t in range(4):
                        project_tile(i + 1, 1 - u, t)
                outputs(i, u, 3)
                if ahead:
                    pe.wait_ge(qkg_s, i * 4 + 8)
                finish(i)

            pe.wait_ge(const_s, 16)
            pe.wait_ge(cleared_s, 4)
            pe.wait_ge(route_w_s, 16)
            for h in range(HALVES):
                route(0, h)
                rank(0, h)
            ffn(0)
            pe.wait_ge(y_s, NB)
            pe.wait_ge(att_w_s, 16 * 8)
            pe.wait_ge(masks_s, 2)
            transpose_batch(0)
            project_dense(0, 0)
            for t in range(4):
                project_tile(0, 0, t)
            for i in range(B):
                attend(i, i % 2, i + 1 < B, i == 0)
                if i == BH + 1:
                    pe.wait_ge(att_s, i + 1)
                    route(1, 0)
                    rank(1, 0)
            pe.wait_ge(att_s, B)
            ffn(1, 4, lambda: (route(1, 1), rank(1, 1)))


def kernel(**inputs):
    import numpy as np
    import concourse.bacc as bacc
    from concourse import mybir as mb
    from concourse.bass_utils import run_bass_kernel_spmd as run

    a = {k.split("_", 1)[1]: np.ascontiguousarray(v) for k, v in inputs.items()}
    wqk, bqk = a["attn_Wqk"], a["attn_bqk"]

    def spread_heads(w):
        z = np.zeros((w.shape[0], 32 - HEAD), w.dtype)
        return np.concatenate([p for h in range(DENSE) for p in (w[:, h * HEAD:(h + 1) * HEAD], z)], axis=1)

    p = np.arange(128)
    key = np.arange(-128, 128)
    lag = p[:, None] - key[None, :]
    off = [np.where((lag >= 0) & (lag < w), 0.0, -BIG) for w in WINDOWS[:DENSE]]
    o = np.arange(7, -1, -1)
    light = np.zeros((128, 4, LIGHT, 8))
    light[:, :, 1:, :SHIFTS] = -BIG
    light[:, 0, :, :] = np.minimum(light[:, 0, :, :], np.where(p[:, None, None] < o[None, None, :], -BIG, 0.0))
    consts = {
        "ident": np.eye(128), "below": np.triu(np.ones((128, 128)), 1),
        "mask_first": np.concatenate([m[:, 128:] for m in off], axis=1),
        "mask_rest": np.concatenate([m[:, 128 - v:] for m, v in zip(off, PREV)], axis=1),
        "light_mask": light.reshape(128, -1),
        "first_of_ties": np.tile(np.arange(E, 0, -1), (128, 1)),
        "block_no": np.tile(np.arange(NBH), (128, 1)),
        "full_blocks": np.tile(128 * np.arange(TH), (128, 1)),
        "head_rows": p[:, None] // 32 == np.arange(DENSE)[None, :],
    }
    consts = np.concatenate([consts[n] for n in CONST], axis=1).astype(np.float32)
    no_bias = np.zeros(HEAD, bqk.dtype)
    b_q4 = np.concatenate([spread_heads(np.concatenate([bqk[h * HEAD:(h + 1) * HEAD] if g == h else no_bias
                                                        for g in range(DENSE)])[None, :]).reshape(128, 1)
                           for h in range(DENSE)], axis=1)
    arrays = {
        "x": a["attn_x"],
        "w_qkg": np.concatenate([wqk, a["attn_Wgate"]], axis=1),
        "b_qkg": np.concatenate([bqk, a["attn_bgate"]])[None, :],
        "w_q4": spread_heads(wqk[:, :C]), "w_k4": spread_heads(wqk[:, C:]),
        "b_q4": b_q4, "b_k4": spread_heads(bqk[None, C:]).reshape(128, 1),
        "w_proj": a["attn_Wproj"], "b_proj": a["attn_bproj"][None, :],
        "w_router": a["ffn_router_w"].T, "w_fc": a["ffn_expert_fc"],
        "w_out": a["ffn_expert_proj"].transpose(0, 2, 1), "consts": consts,
    }
    arrays = {k: np.ascontiguousarray(v) for k, v in arrays.items()}
    nc = bacc.Bacc("TRN2", target_bir_lowering=False, num_devices=1)
    args = [nc.dram_tensor(f"in_{n}", v.shape, mb.dt.from_np(v.dtype), kind="ExternalInput").ap() for n, v in arrays.items()]
    out = nc.dram_tensor("out_rows", (B, T, C), mb.dt.float32, kind="ExternalOutput").ap()
    macaron(nc, *args, out)
    r = run(nc, [{f"in_{n}": v for n, v in arrays.items()}], core_ids=[0])
    return r.results[0]["out_rows"]
```

```python
import concourse.bass as bass
from concourse import mybir
from contextlib import ExitStack

B, T, C = 8, 512, 128
N_TILES = B * T // 128
N_HEADS, HEAD = 16, 8
WINDOWS = [max(4, 128 // 2 ** h) for h in range(N_HEADS)]
DENSE = 4
LIGHT = N_HEADS - DENSE
LC = LIGHT * HEAD
SHIFTS = 4
E, HID = 8, 512
KT = HID // 128
HALVES = 2
TH = N_TILES // HALVES
BH = B // HALVES
NBH = TH + E - 1
NB = HALVES * NBH
SCALE = HEAD ** -0.5
EPS = 1e-5
BIG = 1e30
NP = NB // 2
CROSS = NBH // 2
LQ, DK, LK, GL = 0, LC, LC + DENSE * HEAD, LC + C
QKG = LC + C + N_HEADS
UNITS = 7
RG = 3
GROUPS = -(-TH // RG)
PAD = 8

PREV = [min(w, 128) for w in WINDOWS[:DENSE]]
SCORE_AT = []
for h in range(DENSE):
    SCORE_AT.append((h // 2, 0 if h % 2 == 0 else 128 + PREV[h - 1]))
BANK_COLS = [sum(128 + PREV[h] for h in (0, 1)), sum(128 + PREV[h] for h in (2, 3))]

CONST = {"ident": 128, "below": 128, "mask_first": DENSE * 128, "mask_rest": sum(BANK_COLS),
         "light_mask": 4 * LIGHT * 8, "first_of_ties": E, "block_no": NBH, "full_blocks": TH, "head_scale": DENSE}
CONST_AT, _at = {}, 0
for _n, _w in CONST.items():
    CONST_AT[_n] = (_at, _at + _w)
    _at += _w
CONST_COLS = _at


def macaron(nc, x_in, w_qkg, b_qkg, w_q4, w_k4, b_q4, b_k4, w_proj, b_proj, w_router, w_fc, w_out, consts, out):
    f32, bf16, i32, u32 = mybir.dt.float32, mybir.dt.bfloat16, mybir.dt.int32, mybir.dt.uint32
    ALU, ACT, AX = mybir.AluOpType, mybir.ActivationFunctionType, mybir.AxisListType
    ds = bass.ds
    ctx = ExitStack()
    with ctx:
        def sb(name, shape, dt=f32):
            return ctx.enter_context(nc.sbuf_tensor(name, shape, dt))

        def sem(name):
            return ctx.enter_context(nc.semaphore(name))

        banks01 = ctx.enter_context(nc.psum_tensor("banks01", [128, 1024], f32))
        banks23 = ctx.enter_context(nc.psum_tensor("banks23", [128, 1024], f32))
        bank = [b[:, k * 512:(k + 1) * 512] for b in (banks01, banks23) for k in range(2)]
        bank += [ctx.enter_context(nc.psum_tensor(f"bank{i}", [128, 512], f32))[:, :] for i in range(4, 8)]
        banks01, banks23 = banks01[:, :], banks23[:, :]

        x = sb("x", [128, N_TILES, C])
        xn = sb("xn", [128, N_TILES, C])
        yg = sb("yg", [128, N_TILES, C])
        sq = sb("sq", [128, TH, C])
        rowsum = sb("rowsum", [128, N_TILES])
        var = sb("var", [128, N_TILES])
        rstd = sb("rstd", [128, N_TILES])
        newton = sb("newton", [128, TH])
        fc = sb("fc", [128, E, HID])
        wo = sb("wo", [128, E, KT, C])
        wqkg = sb("wqkg", [128, QKG])
        bqkg = sb("bqkg", [128, QKG])
        wq4 = sb("wq4", [128, 128])
        wk4 = sb("wk4", [128, 128])
        bq4 = sb("bq4", [128, DENSE])
        bk4 = sb("bk4", [128, 1])
        wproj = sb("wproj", [128, C])
        bproj = sb("bproj", [128, C])
        wr = sb("wr", [128, E])
        cst = sb("cst", [128, CONST_COLS])
        ones = sb("ones", [128, 128])
        identb = sb("identb", [128, 128], bf16)
        maskb = sb("maskb", [128, DENSE * 128 + sum(BANK_COLS)], bf16)

        def const(name):
            a, b = CONST_AT[name]
            return cst[:, a:b]

        ident = const("ident")
        top = sb("top", [128, TH])
        top2 = sb("top2", [128, TH])
        tied = sb("tied", [128, TH, E])
        hot = sb("hot", [128, TH, E])
        cnt = sb("cnt", [128, E, TH])
        upto = sb("upto", [128, E, TH])
        before = sb("before", [128, E, TH])
        n_tok = sb("n_tok", [128, E])
        over = sb("over", [128, E, TH])
        n_blk = sb("n_blk", [128, E])
        blk_end = sb("blk_end", [128, E])
        base = sb("base", [128, E])
        place = sb("place", [128, E, TH])
        slot_e = sb("slot_e", [128, TH, E])
        slot_f = sb("slot_f", [128, TH])
        slot = sb("slot", [128, N_TILES], i32)
        rT = sb("rT", [128, 2, RG * 128])
        past = sb("past", [1, NBH, E])
        expert_f = sb("expert_f", [1, NBH])
        expert = sb("expert", [1, NB], i32)
        xs = sb("xs", [128, 2, C])
        xT = sb("xT", [128, 2, 128])
        r = sb("r", [128, 2, HID])
        hT = sb("hT", [128, 2, KT, 128])
        ys = sb("ys", [128, 2, C])
        xb = sb("xb", [128, 4, C])
        xnT = sb("xnT", [128, 2, 4 * 128])
        bq4s = sb("bq4s", [128, DENSE])
        qT = sb("qT", [128, 2, DENSE, 512])
        kT = sb("kT", [128, 2, 512])
        qkg = sb("qkg", [128, 2, 4, QKG])
        ks = sb("ks", [128, 2, SHIFTS, 4, LC])
        ks4 = sb("ks4", [128, 2, SHIFTS, 4, HEAD])
        prod = sb("prod", [128, SHIFTS, 4, LC])
        prod4 = sb("prod4", [128, SHIFTS, 4, HEAD])
        part = sb("part", [128, SHIFTS, 4, LC])
        part4 = sb("part4", [128, SHIFTS, 4, HEAD])
        sc = sb("sc", [128, 8, 4, LIGHT])
        scm = sb("scm", [128, 8 * 4 * LIGHT])
        lmax = sb("lmax", [128, 4 * LIGHT])
        pl = sb("pl", [128, 8 * 4 * LIGHT])
        pl4 = pl[:, :].rearrange("p (s t h) -> p s t h", s=8, t=4)
        osh = sb("osh", [128, 4, LC])
        o4 = sb("o4", [128, 4 * HEAD])
        nmax = sb("nmax", [128, 4, DENSE])
        P = sb("P", [128, 2, DENSE, 256])
        PT = sb("PT", [128, 2, DENSE, 2, 128])
        den = sb("den", [128, 2, 4, N_HEADS])
        gmax = sb("gmax", [128, 4])
        gl = sb("gl", [128, 4, N_HEADS])
        ge = sb("ge", [128, 2, 4, N_HEADS])
        gsum = sb("gsum", [128, 4])
        dg = sb("dg", [128, 4, N_HEADS])
        rc = sb("rc", [128, 4, N_HEADS])
        fac = sb("fac", [128, 4, N_HEADS])
        gated = r[:, 0, :].rearrange("p (t c) -> p t c", t=4)
        gT = r[:, 1, :]

        rows_d = nc.dram_tensor("rows_d", [NB * 128, C], f32, kind="Internal")
        y_d = nc.dram_tensor("y_d", [NB * 128, C], f32, kind="Internal")
        k_d = nc.dram_tensor("k_d", [PAD + B * T, LC], f32, kind="Internal")

        x_v = x_in.rearrange("b t c -> (b t) c").rearrange("(n p) c -> p n c", p=128)
        out_v = out.rearrange("b t c -> (b t) c").rearrange("(n p) c -> p n c", p=128)

        x_in_s = [sem(f"x_loaded{n}") for n in range(HALVES)]
        const_s = sem("constants_loaded")
        route_w_s = sem("router_weights_loaded")
        ffn_w_s = sem("expert_weights_loaded")
        att_w_s = sem("attention_weights_loaded")
        cleared_s = sem("buffers_cleared")
        zero_s = sem("dram_padding_zeroed")
        masks_s = sem("masks_cast")
        step_s = sem("vector_step")
        xres_s = sem("residual_updated")
        cent_s = sem("rows_centred")
        sq_s = sem("squares_ready")
        var_s = sem("squares_summed")
        rstd_s = sem("spread_known")
        norm_s = sem("rows_normalised")
        rt_px_s = sem("route_rows_transposed")
        rt_T_s = sem("route_transposes_copied")
        logit_s = sem("logits_ready")
        hot_s = sem("expert_choice_ready")
        rank_s = sem("ranks_ready")
        slot_s = sem("slots_ready")
        scat_s = [sem(f"rows_scattered{n}") for n in range(HALVES)]
        gath_s = [sem(f"outputs_gathered{n}") for n in range(B)]
        ld_s = sem("pair_loaded")
        st_s = sem("pair_stored")
        px_s = sem("pair_transposed")
        xT_s = sem("pair_transpose_copied")
        h_s = sem("hidden_ready")
        r_s = sem("relu_ready")
        rT_s = sem("relu_transposed")
        hT_s = sem("hidden_squared")
        py_s = sem("pair_output_ready")
        y_s = sem("pair_output_copied")
        bias_s = sem("output_bias_added")
        bq_s = sem("query_bias_scaled")
        xb_s = sem("batch_normalised")
        a_px_s = sem("batch_transposed")
        a_xT_s = sem("batch_transpose_copied")
        q_s = sem("dense_queries_ready")
        k_s = sem("dense_keys_ready")
        qkT_s = sem("dense_qk_copied")
        qkg_p_s = sem("qkg_ready")
        qkg_s = sem("qkg_biased")
        kw_s = sem("keys_written")
        ks_s = [sem(f"shifted_keys_loaded{n}") for n in range(2)]
        s_s = sem("dense_scores_ready")
        nmax_s = sem("dense_max_ready")
        p_s = sem("dense_probs_ready")
        pt_s = sem("dense_probs_transposed")
        ptc_s = sem("dense_probs_copied")
        pv_s = sem("dense_outputs_ready")
        lprod_s = sem("light_products_ready")
        lsc_s = sem("light_scores_ready")
        lp_s = sem("light_probs_ready")
        lpart_s = sem("light_parts_ready")
        gl_s = sem("gate_logits_ready")
        ge_s = sem("gates_ready")
        gated_s = sem("gated_ready")
        gp_s = sem("gated_transposed")
        gT_s = sem("gated_copied")
        proj_s = sem("projection_ready")
        att_s = sem("attention_added")
        out_s = sem("output_stored")

        def span(h):
            return slice(h * TH, (h + 1) * TH)

        def probs_after(i, n):
            return 16 * i + 4 + 2 * n

        def ahead(i, n, k):
            i, n = i + (n + k) // UNITS, (n + k) % UNITS
            return (i, n) if i < B else None

        def unit(n):
            if n == 0:
                return 0, [(h, h * 128, 128) for h in range(DENSE)]
            t, k = (n + 1) // 2, (n - 1) % 2
            return t, [(h, SCORE_AT[h][1], 128 + PREV[h]) for h in (2 * k, 2 * k + 1)]

        block = ctx.enter_context(nc.Block())

        def normalise_batch(eng, i):
            eng.wait_ge(rstd_s, 3 + i // BH)
            if i:
                eng.wait_ge(a_px_s, i)
            eng.tensor_tensor(xb[:, :, :], xn[:, ds(i * 4, 4), :],
                              rstd[:, ds(i * 4, 4)].unsqueeze(2).to_broadcast([128, 4, C]), ALU.mult).then_inc(xb_s, 1)

        def light_products(eng, i, u):
            lq = qkg[:, u, :, LQ:LQ + LC]
            eng.wait_ge(ks_s[u], (i // 2 + 1) * 32 * SHIFTS)
            if i:
                eng.wait_ge(lsc_s, i)
            eng.tensor_tensor(prod4[:, :, :, :], ks4[:, u, :, :, :],
                              lq[:, :, 0:HEAD].unsqueeze(1).to_broadcast([128, SHIFTS, 4, HEAD]), ALU.mult)
            eng.tensor_tensor(prod[:, :, :, :], ks[:, u, :, :, :],
                              lq.unsqueeze(1).to_broadcast([128, SHIFTS, 4, LC]), ALU.mult).then_inc(lprod_s, 1)

        def light_parts(eng, i, u):
            eng.wait_ge(lp_s, i + 1)
            eng.tensor_tensor(part4[:, :, :, :].rearrange("p s t d -> p (s t) d"),
                              ks4[:, u, :, :, :].rearrange("p s t d -> p (s t) d"),
                              pl4[:, 0:SHIFTS, :, 0].rearrange("p s t -> p (s t)").unsqueeze(2).to_broadcast(
                                  [128, SHIFTS * 4, HEAD]), ALU.mult)
            eng.tensor_tensor(part[:, :, :, :].rearrange("p s t (h d) -> p (s t h) d", d=HEAD),
                              ks[:, u, :, :, :].rearrange("p s t (h d) -> p (s t h) d", d=HEAD),
                              pl4[:, SHIFTS:, :, :].rearrange("p s t h -> p (s t h)").unsqueeze(2).to_broadcast(
                                  [128, SHIFTS * 4 * LIGHT, HEAD]), ALU.mult).then_inc(lpart_s, 1)

        @block.sync
        def _(sp):
            for h in range(HALVES):
                sp.dma_start(x[:, span(h), :], x_v[:, span(h), :]).then_inc(x_in_s[h], 16)
                if h == 0:
                    sp.dma_start(cst[:, :], consts).then_inc(const_s, 16)
                    sp.dma_start(wr[:, :], w_router).then_inc(route_w_s, 16)
            sp.wait_ge(cleared_s, 1)
            for h in range(HALVES):
                sp.dma_start(rows_d[h * NBH * 128:(h + 1) * NBH * 128, :].rearrange("(p n) c -> p n c", p=128),
                             yg[:, 0:NBH, :]).then_inc(zero_s, 16)
            sp.dma_start(k_d[0:PAD, :], yg[0:PAD, 0, 0:LC]).then_inc(zero_s, 16)
            sp.dma_start(fc[:, :, :], w_fc.rearrange("e d h -> d e h")).then_inc(ffn_w_s, 16)
            sp.dma_start(wo[:, :, :, :].rearrange("p e k d -> p (e k) d"),
                         w_out.rearrange("e (k p) d -> p (e k) d", p=128)).then_inc(ffn_w_s, 16)
            for dst, src in ((wqkg, w_qkg), (wq4, w_q4), (wk4, w_k4), (bq4, b_q4), (bk4, b_k4), (wproj, w_proj)):
                sp.dma_start(dst[:, :], src).then_inc(att_w_s, 16)
            sp.dma_start(bqkg[:, :], b_qkg.to_broadcast([128, QKG])).then_inc(att_w_s, 16)
            sp.dma_start(bproj[:, :], b_proj.to_broadcast([128, C])).then_inc(att_w_s, 16)

            def load(j):
                sp.dma_start(xs[:, :, :], rows_d[ds(j * 256, 256), :].rearrange("(u p) c -> p u c", p=128)
                             ).then_inc(ld_s, 16)

            def store(j):
                sp.dma_start(y_d[ds(j * 256, 256), :].rearrange("(u p) c -> p u c", p=128), ys[:, :, :]
                             ).then_inc(st_s, 16)

            def ffn(f):
                scattered = 16 * TH * (f + 1)

                def step(j, first=False, last=False):
                    if not last:
                        sp.wait_ge(px_s, j + (NP * f + 2))
                        load(j + 2)
                    if not first:
                        sp.wait_ge(y_s, j + NP * f)
                        store(j - 1)

                sp.wait_ge(scat_s[0], scattered)
                load(0)
                sp.wait_ge(px_s, NP * f + 1)
                load(1)
                step(0, first=True)
                with sp.Fori(1, CROSS - 2) as j:
                    step(j)
                sp.wait_ge(scat_s[1], scattered)
                with sp.Fori(CROSS - 2, NP - 2) as j:
                    step(j)
                step(NP - 2, last=True)
                step(NP - 1, last=True)
                sp.wait_ge(y_s, NP * f + NP)
                store(NP - 1)

            def keys(i, u):
                sp.wait_ge(qkg_s, 2 * i + 2)
                sp.dma_start(k_d[ds(i * T + PAD, T), :].rearrange("(t p) c -> p t c", p=128),
                             qkg[:, u, :, LK:LK + LC]).then_inc(kw_s, 16)
                sp.wait_ge(kw_s, i * 16 + 16)
                for s in range(SHIFTS):
                    sp.dma_start(ks[:, u, s, :, :],
                                 k_d[ds(i * T + (PAD + s + 1 - SHIFTS), T), :].rearrange("(t p) c -> p t c", p=128)
                                 ).then_inc(ks_s[u], 16)
                for s in range(SHIFTS):
                    sp.dma_start(ks4[:, u, s, :, :],
                                 k_d[ds(i * T + (PAD + s + 1 - 2 * SHIFTS), T), 0:HEAD].rearrange(
                                     "(t p) c -> p t c", p=128)).then_inc(ks_s[u], 16)

            ffn(0)
            sp.wait_ge(zero_s, 48)
            for i in range(B):
                keys(i, i % 2)
            ffn(1)
            sp.wait_ge(xres_s, 3)
            sp.dma_start(out_v[:, span(0), :], x[:, span(0), :]).then_inc(out_s, 16)
            for i in range(BH, B):
                sp.wait_ge(xres_s, i - BH + 4)
                sp.dma_start(out_v[:, 4 * i:4 * i + 4, :], x[:, 4 * i:4 * i + 4, :]).then_inc(out_s, 16)
            sp.wait_ge(out_s, 16 * (1 + BH))

        @block.gpsimd
        def _(pool):
            pool.memset(yg[:, 0:NBH, :], 0.0).then_inc(cleared_s, 1)
            pool.memset(ones[:, :], 1.0).then_inc(cleared_s, 1)
            pool.memset(P[:, :, :, :], 0.0).then_inc(cleared_s, 1)
            pool.memset(sc[:, :, :, :], 0.0).then_inc(cleared_s, 1)

            def scatter(f, h):
                pool.wait_ge(slot_s, HALVES * f + h + 1)
                for t in range(h * TH, (h + 1) * TH):
                    pool.indirect_dma_start(
                        out=rows_d[:, :], out_offset=bass.IndirectOffsetOnAxis(ap=slot[:, t:t + 1].bitcast(u32), axis=0),
                        in_=xn[:, t, :], in_offset=None).then_inc(scat_s[h], 16)

            def gather(f, h):
                pool.wait_ge(st_s, 16 * (NP * f + (CROSS + 1 if h == 0 else NP)))
                for t in range(h * TH, (h + 1) * TH):
                    pool.indirect_dma_start(
                        out=yg[:, t, :], out_offset=None, in_=y_d[0:(h + 1) * NBH * 128, :],
                        in_offset=bass.IndirectOffsetOnAxis(ap=slot[:, t:t + 1].bitcast(u32), axis=0)
                    ).then_inc(gath_s[t // 4], 16)

            def squares(n, h):
                pool.wait_ge(cent_s, n + 1)
                pool.wait_ge(var_s, n)
                pool.tensor_tensor(sq[:, :, :], xn[:, span(h), :], xn[:, span(h), :], ALU.mult).then_inc(sq_s, 1)

            def add_output_bias(h):
                pool.wait_ge(att_w_s, 16 * 8)
                pool.tensor_tensor(x[:, span(h), :], x[:, span(h), :],
                                   bproj[:, :].unsqueeze(1).to_broadcast([128, TH, C]), ALU.add).then_inc(bias_s, 1)

            def window(i):
                if i > 0:
                    light_products(pool, i, i % 2)
                if i + 2 < B:
                    normalise_batch(pool, i + 2)
                if i == 1:
                    squares(3, 1)
                if i == BH + 1:
                    squares(4, 0)
                if i + 1 < B:
                    light_parts(pool, i, i % 2)
                if i == 1:
                    add_output_bias(1)

            pool.wait_ge(zero_s, 48)
            scatter(0, 0)
            scatter(0, 1)
            gather(0, 0)
            squares(2, 0)
            add_output_bias(0)
            normalise_batch(pool, 0)
            gather(0, 1)
            for i in range(B):
                window(i)
            scatter(1, 0)
            scatter(1, 1)
            gather(1, 0)
            gather(1, 1)

        @block.scalar
        def _(act):
            act.preload_act_table(ACT.Exp)
            act.wait_ge(const_s, 16)
            act.activation(identb[:, :], ident, ACT.Copy).then_inc(masks_s, 1)
            a, b_ = CONST_AT["mask_first"][0], CONST_AT["mask_rest"][1]
            act.activation(maskb[:, :], cst[:, a:b_], ACT.Copy).then_inc(masks_s, 1)

            def squares(n, h):
                act.wait_ge(cent_s, n + 1)
                if n:
                    act.wait_ge(var_s, n)
                act.activation(sq[:, :, :], xn[:, span(h), :], ACT.Square).then_inc(sq_s, 1)

            def route_copy(f, h, g, b):
                m = (HALVES * f + h) * GROUPS + g
                w = 128 * (min(TH, RG * g + RG) - RG * g)
                act.wait_ge(rt_px_s, m + 1)
                if m >= 2:
                    act.wait_ge(logit_s, m - 1)
                act.activation(rT[:, m % 2, 0:w], bank[b][:, 0:w], ACT.Copy).then_inc(rt_T_s, 1)

            def copy_rows(f, j):
                act.wait_ge(px_s, j + (NP * f + 1))
                act.activation(xT[:, :, :], bank[5][:, 0:256].rearrange("p (u c) -> p u c", u=2), ACT.Copy).then_inc(xT_s, 1)

            def ffn_step(f, j, last=False):
                if not last:
                    copy_rows(f, j + 1)
                act.wait_ge(rT_s, j + (NP * f + 1))
                act.activation(hT[:, :, :, :].rearrange("p u k c -> p (u k c)"), banks23, ACT.Square).then_inc(hT_s, 1)

            def ffn(f, work):
                copy_rows(f, 0)
                j = 0
                for j in range(len(work)):
                    for w in work[j]:
                        w()
                    ffn_step(f, j)
                with act.Fori(len(work), NP - 1) as j:
                    ffn_step(f, j)
                ffn_step(f, NP - 1, last=True)

            def copy_batch(i):
                act.wait_ge(a_px_s, i + 1)
                act.activation(xnT[:, i % 2, :], bank[6][:, :], ACT.Copy).then_inc(a_xT_s, 1)

            def copy_queries(i, heads):
                act.wait_ge(q_s, i + 1)
                for h in heads:
                    act.activation(qT[:, i % 2, h, :], bank[7][:, :], ACT.Identity, bias=bq4s[:, h:h + 1],
                                   scale=const("head_scale")[:, h:h + 1]).then_inc(qkT_s, 1)

            def copy_keys(i):
                act.wait_ge(k_s, i + 1)
                act.activation(kT[:, i % 2, :], bank[6][:, :], ACT.Identity, bias=bk4[:, 0:1]).then_inc(qkT_s, 1)

            def dense_probs(i, n):
                act.wait_ge(nmax_s, UNITS * i + n + 1)
                if n == 1 and i:
                    act.wait_ge(pt_s, UNITS * i)
                t, heads = unit(n)
                for h, a0, w in heads:
                    act.activation(P[:, t % 2, h, 256 - w:256], bank[(n + i) % 2][:, a0:a0 + w], ACT.Exp,
                                   bias=nmax[:, t, h:h + 1], accum_out=den[:, i % 2, t, h:h + 1]).then_inc(p_s, 1)

            def copy_probs(i, n):
                t = (n + 1) // 2
                act.wait_ge(pt_s, UNITS * i + n + 1)
                if 4 * i + t > 1:
                    act.wait_ge(pv_s, 4 * i + t - 1)
                if n == 0:
                    act.activation(PT[:, 0, :, 1, :], bank[3][:, :].rearrange("p (h q) -> p h q", h=DENSE),
                                   ACT.Copy).then_inc(ptc_s, 1)
                else:
                    k = (n - 1) % 2
                    act.activation(PT[:, t % 2, 2 * k:2 * k + 2, :, :].rearrange("p h a q -> p (h a q)"),
                                   bank[3][:, :], ACT.Copy).then_inc(ptc_s, 1)

            def light_probs(i):
                act.wait_ge(lsc_s, i + 1)
                act.activation(pl[:, :], scm[:, :], ACT.Exp, scale=SCALE).then_inc(lp_s, 1)

            def gates(i):
                act.wait_ge(gl_s, i + 1)
                act.activation(ge[:, i % 2, :, :], gl[:, :, :], ACT.Exp).then_inc(ge_s, 1)

            def copy_gated(i):
                act.wait_ge(gp_s, i + 1)
                act.activation(gT, bank[6][:, :], ACT.Copy).then_inc(gT_s, 1)

            def slot_of(i, n):
                nxt = ahead(i, n, 1)
                if nxt:
                    dense_probs(*nxt)
                copy_probs(i, n)
                if i + 1 < B:
                    if n == 0:
                        copy_batch(i + 1)
                    if n in (1, 2):
                        copy_queries(i + 1, (2 * n - 2, 2 * n - 1))
                    if n == 3:
                        copy_keys(i + 1)
                    if n == 6:
                        gates(i + 1)
                if n == 5:
                    light_probs(i)
                    if i:
                        copy_gated(i - 1)
                if i == BH + 2 and n < GROUPS:
                    route_copy(1, 0, n, 2)

            squares(0, 0)
            for g in range(GROUPS):
                route_copy(0, 0, g, 6)
            squares(1, 1)
            for g in range(GROUPS):
                route_copy(0, 1, g, 7)
            ffn(0, [])
            act.wait_ge(att_w_s, 16 * 8)
            act.activation(bq4s[:, :], bq4[:, :], ACT.Copy, scale=SCALE).then_inc(bq_s, 1)
            copy_batch(0)
            act.wait_ge(bq_s, 1)
            copy_queries(0, range(DENSE))
            copy_keys(0)
            gates(0)
            dense_probs(0, 0)
            for i in range(B):
                for n in range(UNITS):
                    slot_of(i, n)
            copy_gated(B - 1)
            squares(5, 1)
            ffn(1, [[], [], [lambda g=g: route_copy(1, 1, g, 6) for g in (0, 1, 2)],
                    [lambda g=g: route_copy(1, 1, g, 6) for g in (3, 4, 5)]])

        @block.vector
        def _(dve):
            steps = [0]

            def step(ins):
                steps[0] += 1
                ins.then_inc(step_s, 1)
                dve.wait_ge(step_s, steps[0])

            def row_sums(h):
                step(nc.vector.tensor_reduce(rowsum[:, span(h)], x[:, span(h), :], AX.X, ALU.add))

            def centre(h):
                nc.vector.scalar_tensor_tensor(
                    xn[:, span(h), :], rowsum[:, span(h)].unsqueeze(2).to_broadcast([128, TH, C]), -1.0 / C,
                    x[:, span(h), :], ALU.mult, ALU.add).then_inc(cent_s, 1)

            def variance(n, h):
                dve.wait_ge(sq_s, n + 1)
                nc.vector.tensor_reduce(var[:, span(h)], sq[:, :, :], AX.X, ALU.add).then_inc(var_s, 1)
                dve.wait_ge(var_s, n + 1)
                step(nc.vector.tensor_scalar(var[:, span(h)], var[:, span(h)], 1.0 / C, EPS, ALU.mult, ALU.add))

            def spread(n, h):
                step(nc.vector.tensor_scalar(rstd[:, span(h)].bitcast(i32), var[:, span(h)].bitcast(i32),
                                             -0.5, float(0x5f3759df), ALU.mult, ALU.add))
                for k in range(3):
                    step(nc.vector.tensor_tensor(newton[:, :], rstd[:, span(h)], rstd[:, span(h)], ALU.mult))
                    step(nc.vector.scalar_tensor_tensor(newton[:, :], newton[:, :], -0.5, var[:, span(h)],
                                                        ALU.mult, ALU.mult))
                    root = nc.vector.scalar_tensor_tensor(rstd[:, span(h)], newton[:, :], 1.5, rstd[:, span(h)],
                                                          ALU.add, ALU.mult)
                    if k < 2:
                        step(root)
                root.then_inc(rstd_s, 1)

            def normalise(n, h):
                dve.wait_ge(rstd_s, n + 1)
                nc.vector.tensor_tensor(xn[:, span(h), :], xn[:, span(h), :],
                                        rstd[:, span(h)].unsqueeze(2).to_broadcast([128, TH, C]),
                                        ALU.mult).then_inc(norm_s, 1)

            def choose(f, h, b):
                n = HALVES * f + h
                logits = bank[b][:, 384:384 + TH * E].rearrange("p (t e) -> p t e", e=E)

                def along(ap):
                    return ap.unsqueeze(2).to_broadcast([128, TH, E])

                dve.wait_ge(logit_s, GROUPS * (n + 1))
                step(nc.vector.tensor_reduce(top[:, :], logits, AX.X, ALU.max))
                step(nc.vector.tensor_tensor(tied[:, :, :], logits, along(top[:, :]), ALU.is_equal))
                step(nc.vector.tensor_tensor(tied[:, :, :], tied[:, :, :],
                                             const("first_of_ties").unsqueeze(1).to_broadcast([128, TH, E]), ALU.mult))
                step(nc.vector.tensor_reduce(top2[:, :], tied[:, :, :], AX.X, ALU.max))
                nc.vector.tensor_tensor(hot[:, :, :], tied[:, :, :], along(top2[:, :]),
                                        ALU.is_equal).then_inc(hot_s, 1)

            def count_blocks(f, h, b):
                counts = bank[b][:, 128:128 + TH * E].rearrange("p (t e) -> p e t", e=E)
                flat = lambda a: a[:, :, :].rearrange("p e t -> p (e t)")
                dve.wait_ge(rank_s, HALVES * f + h + 1)
                step(nc.vector.tensor_copy(cnt[:, :, :], counts))
                step(nc.vector.tensor_tensor_scan(flat(upto), ones[:, :], flat(cnt), 0.0, ALU.mult, ALU.add))
                step(nc.vector.tensor_tensor(before[:, :, :], upto[:, :, :], cnt[:, :, :], ALU.subtract))
                step(nc.vector.tensor_tensor(n_tok[:, :], upto[:, :, TH - 1], before[:, :, 0], ALU.subtract))
                step(nc.vector.tensor_tensor(over[:, :, :], n_tok[:, :].unsqueeze(2).to_broadcast([128, E, TH]),
                                             const("full_blocks").unsqueeze(1).to_broadcast([128, E, TH]), ALU.is_gt))
                step(nc.vector.tensor_reduce(n_blk[:, :], over[:, :, :], AX.X, ALU.add))
                step(nc.vector.tensor_tensor_scan(blk_end[:, :], ones[:, 0:E], n_blk[:, :], 0.0, ALU.mult, ALU.add))

            def place_blocks(f, h):
                step(nc.vector.tensor_tensor(base[:, :], blk_end[:, :], n_blk[:, :], ALU.subtract))
                step(nc.vector.scalar_tensor_tensor(base[:, :], base[:, :], 128.0, before[:, :, 0],
                                                    ALU.mult, ALU.subtract))
                step(nc.vector.tensor_tensor(past[:, :, :], const("block_no")[0:1, :].unsqueeze(2).to_broadcast([1, NBH, E]),
                                             blk_end[0:1, :].unsqueeze(1).to_broadcast([1, NBH, E]), ALU.is_ge))
                step(nc.vector.tensor_reduce(expert_f[:, :], past[:, :, :], AX.X, ALU.add))
                step(nc.vector.tensor_scalar(expert[:, h * NBH:(h + 1) * NBH], expert_f[:, :], float(E - 1), None, ALU.min))

            def place_tokens(f, h, b):
                ranks = bank[b][:, 0:TH * E].rearrange("p (t e) -> p t e", e=E)
                step(nc.vector.tensor_tensor(place[:, :, :], before[:, :, :],
                                             base[:, :].unsqueeze(2).to_broadcast([128, E, TH]), ALU.add))
                step(nc.vector.tensor_tensor(slot_e[:, :, :], place[:, :, :].rearrange("p e t -> p t e"), ranks, ALU.add))
                step(nc.vector.tensor_tensor(slot_e[:, :, :], slot_e[:, :, :], hot[:, :, :], ALU.mult))
                step(nc.vector.tensor_reduce(slot_f[:, :], slot_e[:, :, :], AX.X, ALU.add))
                nc.vector.tensor_scalar(slot[:, span(h)], slot_f[:, :], float(h * NBH * 128), None,
                                        ALU.add).then_inc(slot_s, 1)

            def relu(f, j):
                dve.wait_ge(h_s, j + (NP * f + 1))
                nc.vector.tensor_scalar(r[:, :, :].rearrange("p u h -> p (u h)"), banks01, 0.0, None,
                                        ALU.max).then_inc(r_s, 1)

            def copy_out(f, j, first=False):
                dve.wait_ge(py_s, j + (NP * f + 1))
                if f or not first:
                    dve.wait_ge(st_s, (j + NP * f) * 16)
                nc.vector.tensor_copy(ys[:, :, :], bank[4][:, 0:256].rearrange("p (u c) -> p u c", u=2)).then_inc(y_s, 1)

            def ffn(f, work):
                j = 0
                while j < NP:
                    if j > 1 and j not in work:
                        end = min([k for k in work if k > j] + [NP])
                        with dve.Fori(j, end) as q:
                            relu(f, q)
                            copy_out(f, q - 1)
                        j = end
                        continue
                    relu(f, j)
                    if j:
                        copy_out(f, j - 1, first=j == 1)
                    for w in work.get(j, ()):
                        w()
                    j += 1
                copy_out(f, NP - 1)

            def residual(f, tiles, n):
                for g in range(tiles.start // 4, tiles.stop // 4):
                    dve.wait_ge(gath_s[g], 64 * (f + 1))
                nc.vector.scalar_tensor_tensor(x[:, tiles, :], yg[:, tiles, :], 0.5, x[:, tiles, :],
                                               ALU.mult, ALU.add).then_inc(xres_s, 1)
                dve.wait_ge(xres_s, n)

            def add_bias(i, k):
                dve.wait_ge(qkg_p_s, 2 * i + k + 1)
                nc.vector.tensor_tensor(qkg[:, i % 2, 2 * k:2 * k + 2, :],
                                        bank[5][:, 0:2 * QKG].rearrange("p (t c) -> p t c", t=2),
                                        bqkg[:, :].unsqueeze(1).to_broadcast([128, 2, QKG]), ALU.add).then_inc(qkg_s, 1)

            def dense_max(i, n):
                dve.wait_ge(s_s, UNITS * i + n + 1)
                t, heads = unit(n)
                s = bank[(n + i) % 2]
                if n == 0:
                    mx = nc.vector.tensor_reduce(nmax[:, 0, :], s[:, :].rearrange("p (h k) -> p h k", h=DENSE),
                                                 AX.X, ALU.max, negate=True)
                else:
                    for h, a0, w in heads:
                        mx = nc.vector.tensor_reduce(nmax[:, t, h:h + 1], s[:, a0:a0 + w], AX.X, ALU.max, negate=True)
                mx.then_inc(nmax_s, 1)

            def light_sums(i):
                dve.wait_ge(lprod_s, i + 1)
                nc.vector.tensor_reduce(sc[:, 0:SHIFTS, :, 0].rearrange("p s t -> p (s t)"),
                                        prod4[:, :, :, :].rearrange("p s t d -> p (s t) d"), AX.X, ALU.add)
                step(nc.vector.tensor_reduce(sc[:, SHIFTS:, :, :].rearrange("p s t h -> p (s t) h"),
                                             prod[:, :, :, :].rearrange("p s t (h d) -> p (s t) h d", d=HEAD),
                                             AX.X, ALU.add))

            def light_scores(i):
                step(nc.vector.tensor_tensor(scm[:, :], sc[:, :, :, :].rearrange("p s t h -> p (s t h)"),
                                             const("light_mask"), ALU.add))
                scm_s = scm[:, :].rearrange("p (s a) -> p s a", s=8)
                step(nc.vector.tensor_reduce(lmax[:, :], scm_s.rearrange("p s a -> p a s"), AX.X, ALU.max))
                nc.vector.tensor_tensor(scm_s, scm_s, lmax[:, :].unsqueeze(1).to_broadcast([128, 8, 4 * LIGHT]),
                                        ALU.subtract).then_inc(lsc_s, 1)

            def gate_logits(i):
                g = qkg[:, i % 2, :, GL:]
                dve.wait_ge(qkg_s, 2 * i + 2)
                if i:
                    dve.wait_ge(ge_s, i)
                step(nc.vector.tensor_reduce(gmax[:, :], g, AX.X, ALU.max))
                nc.vector.tensor_tensor(gl[:, :, :], g, gmax[:, :].unsqueeze(2).to_broadcast([128, 4, N_HEADS]),
                                        ALU.subtract).then_inc(gl_s, 1)

            def over_d(a):
                return a.unsqueeze(a.ndim).to_broadcast(list(a.shape) + [HEAD])

            def light_outputs(i):
                dve.wait_ge(lpart_s, i + 1)
                nc.vector.tensor_reduce(o4[:, :], part4[:, :, :, :].rearrange("p s t d -> p (t d) s"), AX.X, ALU.add)
                nc.vector.tensor_reduce(den[:, i % 2, :, DENSE:], pl4.rearrange("p s t h -> p t h s"), AX.X, ALU.add)
                step(nc.vector.tensor_reduce(osh[:, :, :].rearrange("p t c -> p (t c)"),
                                             part[:, :, :, :].rearrange("p s t c -> p (t c) s"), AX.X, ALU.add))
                step(nc.vector.tensor_tensor(osh[:, :, 0:HEAD], osh[:, :, 0:HEAD],
                                             o4[:, :].rearrange("p (t d) -> p t d", d=HEAD), ALU.add))

            def gate(i):
                u = i % 2
                dve.wait_ge(ge_s, i + 1)
                step(nc.vector.tensor_reduce(gsum[:, :], ge[:, u, :, :], AX.X, ALU.add))
                dve.wait_ge(p_s, probs_after(i, UNITS - 1))
                step(nc.vector.tensor_tensor(dg[:, :, :], den[:, u, :, :],
                                             gsum[:, :].unsqueeze(2).to_broadcast([128, 4, N_HEADS]), ALU.mult))
                step(nc.vector.reciprocal(rc[:, :, :], dg[:, :, :]))
                step(nc.vector.tensor_tensor(fac[:, :, :], ge[:, u, :, :], rc[:, :, :], ALU.mult))
                if i:
                    dve.wait_ge(gp_s, i)
                nc.vector.tensor_tensor(gated[:, :, DENSE * HEAD:].rearrange("p t (h d) -> p t h d", d=HEAD),
                                        osh[:, :, :].rearrange("p t (h d) -> p t h d", d=HEAD),
                                        over_d(fac[:, :, DENSE:]), ALU.mult)
                dve.wait_ge(pv_s, 4 * i + 4)
                nc.vector.tensor_tensor(gated[:, :, 0:DENSE * HEAD].rearrange("p t (h d) -> p t h d", d=HEAD),
                                        bank[4][:, 0:4 * DENSE * HEAD].rearrange("p (t h d) -> p t h d", t=4, d=HEAD),
                                        over_d(fac[:, :, 0:DENSE]), ALU.mult).then_inc(gated_s, 1)

            def attended(i):
                dve.wait_ge(proj_s, i + 1)
                dve.wait_ge(bias_s, i // BH + 1)
                nc.vector.tensor_tensor(x[:, ds(i * 4, 4), :], bank[7][:, :].rearrange("p (t c) -> p t c", t=4),
                                        x[:, ds(i * 4, 4), :], ALU.add).then_inc(att_s, 1)

            besides = {
                (0, 2): lambda: light_products(nc.vector, 0, 0),
                (1, 0): lambda: residual(0, span(1), 2),
                (1, 1): lambda: row_sums(1), (1, 2): lambda: centre(1),
                (1, 5): lambda: variance(3, 1), (1, 6): lambda: spread(3, 1),
                (BH + 1, 0): lambda: (dve.wait_ge(att_s, BH), row_sums(0)), (BH + 1, 1): lambda: centre(0),
                (BH + 1, 5): lambda: (variance(4, 0), spread(4, 0)), (BH + 1, 6): lambda: normalise(4, 0),
                (BH + 3, 0): lambda: choose(1, 0, 2), (BH + 3, 2): lambda: count_blocks(1, 0, 2),
                (BH + 3, 3): lambda: place_blocks(1, 0), (BH + 3, 4): lambda: place_tokens(1, 0, 2),
            }

            def slot_of(i, n):
                nxt = ahead(i, n, 2)
                if nxt:
                    dense_max(*nxt)
                if i:
                    if n == 0:
                        light_outputs(i - 1)
                    if n == 1:
                        gate(i - 1)
                    if n == 6:
                        attended(i - 1)
                if n == 3:
                    light_sums(i)
                if i + 1 < B:
                    if n in (2, 4):
                        add_bias(i + 1, n // 2 - 1)
                    if n == 5:
                        gate_logits(i + 1)
                if n == 4:
                    light_scores(i)
                if (i, n) in besides:
                    besides[i, n]()

            dve.wait_ge(const_s, 16)
            dve.wait_ge(cleared_s, 4)
            dve.wait_ge(x_in_s[0], 16)
            row_sums(0)
            centre(0)
            variance(0, 0)
            spread(0, 0)
            normalise(0, 0)
            dve.wait_ge(x_in_s[1], 16)
            row_sums(1)
            centre(1)
            choose(0, 0, 6)
            count_blocks(0, 0, 6)
            place_blocks(0, 0)
            place_tokens(0, 0, 6)
            variance(1, 1)
            spread(1, 1)
            normalise(1, 1)
            choose(0, 1, 7)
            count_blocks(0, 1, 7)
            place_blocks(0, 1)
            place_tokens(0, 1, 7)
            ffn(0, {NP - 6: [lambda: residual(0, span(0), 1)], NP - 5: [lambda: row_sums(0)], NP - 4: [lambda: centre(0)],
                    NP - 2: [lambda: variance(2, 0)], NP - 1: [lambda: spread(2, 0)]})
            dve.wait_ge(att_w_s, 16 * 8)
            add_bias(0, 0)
            normalise_batch(nc.vector, 1)
            add_bias(0, 1)
            gate_logits(0)
            dense_max(0, 0)
            dense_max(0, 1)
            for i in range(B):
                for n in range(UNITS):
                    slot_of(i, n)
            light_parts(nc.vector, B - 1, (B - 1) % 2)
            light_outputs(B - 1)
            gate(B - 1)
            attended(B - 1)
            dve.wait_ge(att_s, B)
            row_sums(1)
            centre(1)
            ffn(1, {0: [lambda: variance(5, 1)], 1: [lambda: spread(5, 1), lambda: normalise(5, 1)],
                    3: [lambda: choose(1, 1, 6)],
                    5: [lambda: count_blocks(1, 1, 6), lambda: place_blocks(1, 1), lambda: place_tokens(1, 1, 6)],
                    NP - 5: [lambda: residual(1, span(0), 3)]})
            for i in range(BH, B):
                residual(1, slice(4 * i, 4 * i + 4), i - BH + 4)

        @block.tensor
        def _(pe):
            def route_turn(f, h, g, b):
                n = HALVES * f + h
                if g == 0:
                    pe.wait_ge(norm_s, n + 1)
                for k, t in enumerate(range(RG * g, min(TH, RG * g + RG))):
                    mm = pe.transpose(bank[b][:, k * 128:(k + 1) * 128], xn[:, h * TH + t, :], ident)
                mm.then_inc(rt_px_s, 1)

            def route_logits(f, h, g, b):
                m = (HALVES * f + h) * GROUPS + g
                pe.wait_ge(rt_T_s, m + 1)
                for k, t in enumerate(range(RG * g, min(TH, RG * g + RG))):
                    mm = pe.matmul(bank[b][:, 384 + t * E:384 + t * E + E], rT[:, m % 2, k * 128:(k + 1) * 128], wr[:, :],
                                   start=True, stop=True)
                mm.then_inc(logit_s, 1)

            def route(f, h, groups, b):
                for g in groups:
                    route_turn(f, h, g, b)
                    route_logits(f, h, g, b)

            def rank(f, h, b):
                pe.wait_ge(hot_s, HALVES * f + h + 1)
                choice = hot[:, :, :].rearrange("p t e -> p (t e)")
                pe.matmul(bank[b][:, 0:128], const("below"), choice, start=True, stop=True)
                pe.matmul(bank[b][:, 128:256], ones[:, :], choice, start=True, stop=True).then_inc(rank_s, 1)

            now = [pe.alloc_register(f"expert_now{v}") for v in range(2)]
            then = [pe.alloc_register(f"expert_before{v}") for v in range(2)]

            def expert_of(reg):
                return pe.snap(reg, min_val=0, max_val=E - 1)

            def turn_rows(f, j):
                pe.wait_ge(ld_s, (j + (NP * f + 1)) * 16)
                for v in range(2):
                    mm = pe.transpose(bank[5][:, v * 128:(v + 1) * 128], xs[:, v, :], ident)
                mm.then_inc(px_s, 1)

            def second_products(f, j, settled=True):
                pe.wait_ge(hT_s, j + (NP * f + 1))
                if settled:
                    pe.wait_ge(y_s, j + NP * f)
                for v in range(2):
                    for k in range(KT):
                        mm = pe.matmul(bank[4][:, v * 128:(v + 1) * 128], hT[:, v, k, :], wo[:, ds(expert_of(then[v]), 1), k, :],
                                       start=(k == 0), stop=(k == KT - 1))
                mm.then_inc(py_s, 1)

            def ffn_step(f, j, first=False, second=False, last=False):
                for v in range(2):
                    pe.reg_load(now[v], expert[0:1, ds(2 * j + v, 1)])
                pe.wait_ge(xT_s, j + (NP * f + 1))
                for v in range(2):
                    mm = pe.matmul(bank[v][:, :], xT[:, v, :], fc[:, ds(expert_of(now[v]), 1), :], start=True, stop=True)
                mm.then_inc(h_s, 1)
                if not last:
                    turn_rows(f, j + 1)
                if not first:
                    second_products(f, j - 1, settled=f or not second)
                for v in range(2):
                    pe.reg_mov(then[v], now[v])
                pe.wait_ge(r_s, j + (NP * f + 1))
                for v in range(2):
                    for k in range(KT):
                        mm = pe.transpose(bank[2 + v][:, k * 128:(k + 1) * 128], r[:, v, k * 128:(k + 1) * 128], ident)
                mm.then_inc(rT_s, 1)

            def ffn(f, work):
                pe.wait_ge(ffn_w_s, 32)
                turn_rows(f, 0)
                lo = max([2] + [j + 1 for j in work])
                for j in range(lo):
                    for w in work.get(j, ()):
                        w()
                    ffn_step(f, j, first=j == 0, second=j == 1)
                with pe.Fori(lo, NP - 1) as j:
                    ffn_step(f, j)
                ffn_step(f, NP - 1, last=True)
                second_products(f, NP - 1)

            def turn_batch(i):
                pe.wait_ge(xb_s, i + 1)
                if i >= 3:
                    pe.wait_ge(gT_s, i - 2)
                for t in range(4):
                    mm = pe.transpose(bank[6][:, t * 128:(t + 1) * 128], xb[:, t, :], ident)
                mm.then_inc(a_px_s, 1)

            def dense_queries(i):
                pe.wait_ge(a_xT_s, i + 1)
                if i >= 3:
                    pe.wait_ge(att_s, i - 2)
                pe.matmul(bank[7][:, :], wq4[:, :], xnT[:, i % 2, :], start=True, stop=True).then_inc(q_s, 1)

            def dense_keys(i):
                pe.matmul(bank[6][:, :], wk4[:, :], xnT[:, i % 2, :], start=True, stop=True).then_inc(k_s, 1)

            def project_tiles(i, k):
                if 2 * i + k:
                    pe.wait_ge(qkg_s, 2 * i + k)
                for v in range(2):
                    t = 2 * k + v
                    mm = pe.matmul(bank[5][:, v * QKG:(v + 1) * QKG], xnT[:, i % 2, t * 128:(t + 1) * 128], wqkg[:, :],
                                   start=True, stop=True)
                mm.then_inc(qkg_p_s, 1)

            def scores(i, n):
                if n == 0:
                    pe.wait_ge(qkT_s, (DENSE + 1) * (i + 1))
                back = ahead(i, n, -2)
                if back[0] >= 0:
                    pe.wait_ge(p_s, probs_after(*back))
                t, heads = unit(n)
                s, u = bank[(n + i) % 2], i % 2
                cols = heads[-1][1] + heads[-1][2]
                a = 0 if n == 0 else DENSE * 128 + ((n - 1) % 2) * BANK_COLS[0]
                pe.matmul(s[:, 0:cols], identb[:, :], maskb[:, a:a + cols], start=True, stop=False)
                for h, a0, w in heads:
                    mm = pe.matmul(s[:, a0:a0 + w], qT[:, u, h, t * 128:(t + 1) * 128],
                                   kT[:, u, (t + 1) * 128 - w:(t + 1) * 128], start=False, stop=h == heads[-1][0])
                mm.then_inc(s_s, 1)

            def turn_probs(i, n):
                pe.wait_ge(p_s, probs_after(i, n))
                if UNITS * i + n:
                    pe.wait_ge(ptc_s, UNITS * i + n)
                t, heads = unit(n)
                for c in range(4):
                    if n == 0:
                        src = P[:, 0, c, 128:256]
                    else:
                        src = P[:, t % 2, heads[c // 2][0], 128 * (c % 2):128 * (c % 2) + 128]
                    mm = pe.transpose(bank[3][:, c * 128:(c + 1) * 128], src, ident)
                mm.then_inc(pt_s, 1)

            def outputs(i, t):
                pe.wait_ge(ptc_s, UNITS * i + 2 * t + 1)
                if t == 0:
                    pe.wait_ge(qkg_s, 2 * i + 2)
                    if i:
                        pe.wait_ge(gated_s, i)
                u = i % 2
                for h in range(DENSE):
                    o = bank[4][:, (t * DENSE + h) * HEAD:(t * DENSE + h + 1) * HEAD]
                    v = slice(DK + h * HEAD, DK + (h + 1) * HEAD)
                    mm = pe.matmul(o, PT[:, t % 2, h, 1, :], qkg[:, u, t, v], start=True, stop=(t == 0))
                    if t:
                        mm = pe.matmul(o, PT[:, t % 2, h, 0, :], qkg[:, u, t - 1, v], start=False, stop=True)
                mm.then_inc(pv_s, 1)

            def turn_gated(i):
                pe.wait_ge(gated_s, i + 1)
                pe.wait_ge(qkT_s, (DENSE + 1) * min(i + 3, B))
                for t in range(4):
                    mm = pe.transpose(bank[6][:, t * 128:(t + 1) * 128], gated[:, t, :], ident)
                mm.then_inc(gp_s, 1)

            def project(i):
                pe.wait_ge(gT_s, i + 1)
                for t in range(4):
                    mm = pe.matmul(bank[7][:, t * 128:(t + 1) * 128], gT[:, t * 128:(t + 1) * 128], wproj[:, :],
                                   start=True, stop=True)
                mm.then_inc(proj_s, 1)

            def slot_of(i, n):
                nxt = ahead(i, n, 2)
                if nxt:
                    scores(*nxt)
                if n == 0 and i:
                    outputs(i - 1, 3)
                if n == 3:
                    outputs(i, 0)
                    outputs(i, 1)
                if n == 5:
                    outputs(i, 2)
                turn_probs(i, n)
                if i + 1 < B:
                    if n == 0:
                        turn_batch(i + 1)
                    if n == 1:
                        dense_queries(i + 1)
                        project_tiles(i + 1, 0)
                    if n == 2:
                        dense_keys(i + 1)
                    if n == 3:
                        project_tiles(i + 1, 1)
                if i:
                    if n == 4:
                        turn_gated(i - 1)
                    if n == 5:
                        project(i - 1)
                if i == BH + 2:
                    if 0 < n <= GROUPS:
                        route_logits(1, 0, n - 1, 2)
                    if n < GROUPS:
                        route_turn(1, 0, n, 2)
                if (i, n) == (BH + 3, 1):
                    rank(1, 0, 2)

            pe.wait_ge(const_s, 16)
            pe.wait_ge(cleared_s, 4)
            pe.wait_ge(route_w_s, 16)
            for h in range(HALVES):
                route(0, h, range(GROUPS), 6 + h)
                rank(0, h, 6 + h)
            ffn(0, {})
            pe.wait_ge(y_s, NP)
            pe.wait_ge(att_w_s, 16 * 8)
            pe.wait_ge(masks_s, 2)
            turn_batch(0)
            dense_queries(0)
            dense_keys(0)
            for k in range(2):
                project_tiles(0, k)
            scores(0, 0)
            scores(0, 1)
            for i in range(B):
                for n in range(UNITS):
                    slot_of(i, n)
            outputs(B - 1, 3)
            turn_gated(B - 1)
            project(B - 1)
            ffn(1, {2: [lambda: route(1, 1, (0, 1, 2), 6)], 3: [lambda: route(1, 1, (3, 4, 5), 6)],
                    5: [lambda: rank(1, 1, 6)]})


def kernel(**inputs):
    import numpy as np
    import concourse.bacc as bacc
    from concourse import mybir as mb
    from concourse.bass_utils import run_bass_kernel_spmd as run

    a = {k.split("_", 1)[1]: np.ascontiguousarray(v) for k, v in inputs.items()}
    wqk, bqk = a["attn_Wqk"], a["attn_bqk"]

    def spread_heads(w):
        z = np.zeros((w.shape[0], 32 - HEAD), w.dtype)
        return np.concatenate([p for h in range(DENSE) for p in (w[:, h * HEAD:(h + 1) * HEAD], z)], axis=1)

    p = np.arange(128)
    key = np.arange(-128, 128)
    lag = p[:, None] - key[None, :]
    off = [np.where((lag >= 0) & (lag < w), 0.0, -BIG) for w in WINDOWS[:DENSE]]
    o = np.arange(7, -1, -1)
    light = np.zeros((128, 8, 4, LIGHT))
    light[:, :SHIFTS, :, 1:] = -BIG
    light[:, :, 0, :] = np.minimum(light[:, :, 0, :], np.where(p[:, None, None] < o[None, :, None], -BIG, 0.0))
    consts = {
        "ident": np.eye(128), "below": np.triu(np.ones((128, 128)), 1),
        "mask_first": np.concatenate([m[:, 128:] for m in off], axis=1),
        "mask_rest": np.concatenate([m[:, 128 - v:] for m, v in zip(off, PREV)], axis=1),
        "light_mask": light.reshape(128, -1),
        "first_of_ties": np.tile(np.arange(E, 0, -1), (128, 1)),
        "block_no": np.tile(np.arange(NBH), (128, 1)),
        "full_blocks": np.tile(128 * np.arange(TH), (128, 1)),
        "head_scale": SCALE * (p[:, None] // 32 == np.arange(DENSE)[None, :]),
    }
    consts = np.concatenate([consts[n] for n in CONST], axis=1).astype(np.float32)
    no_bias = np.zeros(HEAD, bqk.dtype)
    b_q4 = np.concatenate([spread_heads(np.concatenate([bqk[h * HEAD:(h + 1) * HEAD] if g == h else no_bias
                                                        for g in range(DENSE)])[None, :]).reshape(128, 1)
                           for h in range(DENSE)], axis=1)
    arrays = {
        "x": a["attn_x"],
        "w_qkg": np.concatenate([wqk[:, DENSE * HEAD:], a["attn_Wgate"]], axis=1),
        "b_qkg": np.concatenate([bqk[DENSE * HEAD:], a["attn_bgate"]])[None, :],
        "w_q4": spread_heads(wqk[:, :C]), "w_k4": spread_heads(wqk[:, C:]),
        "b_q4": b_q4, "b_k4": spread_heads(bqk[None, C:]).reshape(128, 1),
        "w_proj": a["attn_Wproj"], "b_proj": a["attn_bproj"][None, :],
        "w_router": a["ffn_router_w"].T, "w_fc": a["ffn_expert_fc"],
        "w_out": a["ffn_expert_proj"].transpose(0, 2, 1), "consts": consts,
    }
    arrays = {k: np.ascontiguousarray(v) for k, v in arrays.items()}
    nc = bacc.Bacc("TRN2", target_bir_lowering=False, num_devices=1)
    args = [nc.dram_tensor(f"in_{n}", v.shape, mb.dt.from_np(v.dtype), kind="ExternalInput").ap() for n, v in arrays.items()]
    out = nc.dram_tensor("out_rows", (B, T, C), mb.dt.float32, kind="ExternalOutput").ap()
    macaron(nc, *args, out)
    r = run(nc, [{f"in_{n}": v for n, v in arrays.items()}], core_ids=[0])
    return r.results[0]["out_rows"]
```

```python
import concourse.bass as bass
from concourse import mybir
from contextlib import ExitStack

B, T, C = 8, 512, 128
N_TILES = B * T // 128
N_HEADS, HEAD = 16, 8
WINDOWS = [max(4, 128 // 2 ** h) for h in range(N_HEADS)]
DENSE = 4
LIGHT = N_HEADS - DENSE
LC = LIGHT * HEAD
SHIFTS = 4
E, HID = 8, 512
KT = HID // 128
SEG = ((slice(0, 12), slice(12, N_TILES)), (slice(0, 20), slice(20, N_TILES)))
SEG_TILES = [[s.stop - s.start for s in segs] for segs in SEG]
MOST = max(max(n) for n in SEG_TILES)
NBS = [[n + E - 1 for n in ns] for ns in SEG_TILES]
BLOCK0 = [(0, n[0]) for n in NBS]
NB = sum(NBS[0])
SCALE = HEAD ** -0.5
EPS = 1e-5
BIG = 1e30
NP = NB // 2
CROSS = [n[0] // 2 for n in NBS]
LQ, DK, LK, GL = 0, LC, LC + DENSE * HEAD, LC + C
QKG = LC + C + N_HEADS
UNITS = 7
RG = 2
GROUPS = N_TILES // RG
LN1 = (slice(0, 6), slice(6, 12), slice(12, 22), slice(22, N_TILES))
LN2 = (slice(0, 12), slice(12, 20), slice(20, N_TILES))
LN_TILES = max(s.stop - s.start for s in (*LN1, *LN2))
OUT_BANK = (2, 6)
ROW = 2 * C + 1
NO_TOKEN = 2.0
PAD = 8

PREV = [min(w, 128) for w in WINDOWS[:DENSE]]
SCORE_AT = []
for h in range(DENSE):
    SCORE_AT.append((h // 2, 0 if h % 2 == 0 else 128 + PREV[h - 1]))
BANK_COLS = [sum(128 + PREV[h] for h in (0, 1)), sum(128 + PREV[h] for h in (2, 3))]

SLOTS = DENSE + 2
SIDE = [sum(PREV[1:h]) for h in range(DENSE)]

CONST = {"ident": 128, "below": 128, "first_of_ties": E, "block_no": max(max(n) for n in NBS), "full_blocks": MOST,
         "token": N_TILES, "head_scale": DENSE, "mask_first": DENSE * 128, "mask_rest": sum(BANK_COLS), "light_mask": LIGHT * 8}
CONST_AT, _at = {}, 0
for _n, _w in CONST.items():
    CONST_AT[_n] = (_at, _at + _w)
    _at += _w
CONST_COLS = _at
SOON = CONST_AT["mask_first"][0]


def macaron(nc, x_in, w_qkg, b_qkg, w_q4, w_k4, b_q4, b_k4, w_proj, b_proj, w_router, w_fc, w_out, consts, out):
    f32, bf16, i32, u32 = mybir.dt.float32, mybir.dt.bfloat16, mybir.dt.int32, mybir.dt.uint32
    ALU, ACT, AX = mybir.AluOpType, mybir.ActivationFunctionType, mybir.AxisListType
    ds = bass.ds
    ctx = ExitStack()
    with ctx:
        def sb(name, shape, dt=f32):
            return ctx.enter_context(nc.sbuf_tensor(name, shape, dt))

        def sem(name):
            return ctx.enter_context(nc.semaphore(name))

        bank = [ctx.enter_context(nc.psum_tensor(f"bank{i}", [128, 512], f32)) for i in range(8)]

        rows = sb("rows", [128, N_TILES, ROW])
        xn, x, token = rows[:, :, 0:C], rows[:, :, C:2 * C], rows[:, :, 2 * C]
        late = sb("late", [128, N_TILES * C + 2 * DENSE * 256])
        yg = late[:, 0:N_TILES * C].rearrange("p (n c) -> p n c", c=C)
        P = late[:, N_TILES * C:].rearrange("p (u s k) -> p u s k", u=2, k=128)
        xid = late[:, 0:NB * (C + 1)].rearrange("p (n c) -> p n c", c=C + 1)
        sq = sb("sq", [128, LN_TILES, C])
        rowsum = sb("rowsum", [128, N_TILES])
        var = sb("var", [128, N_TILES])
        rstd = sb("rstd", [128, N_TILES])
        newton = sb("newton", [128, MOST])
        fc = sb("fc", [128, E, HID])
        wo = sb("wo", [128, E, KT, C])
        wqkg = sb("wqkg", [128, QKG])
        bqkg = sb("bqkg", [128, QKG])
        wq4 = sb("wq4", [128, 128])
        wk4 = sb("wk4", [128, 128])
        bq4 = sb("bq4", [128, DENSE])
        bk4 = sb("bk4", [128, 1])
        wproj = sb("wproj", [128, C])
        bproj = sb("bproj", [128, C])
        wr = sb("wr", [128, E])
        cst = sb("cst", [128, CONST_COLS])
        ones = sb("ones", [128, max(128, E * MOST)])
        identb = sb("identb", [128, 128], bf16)
        maskb = sb("maskb", [128, DENSE * 128 + sum(BANK_COLS)], bf16)

        def const(name):
            a, b = CONST_AT[name]
            return cst[:, a:b]

        ident = const("ident")
        top = sb("top", [128, MOST])
        top2 = sb("top2", [128, MOST])
        tied = sb("tied", [128, MOST, E])
        hot = sb("hot", [128, MOST, E])
        cnt = sb("cnt", [128, E * MOST])
        upto = sb("upto", [128, E * MOST])
        before = sb("before", [128, E * MOST])
        over = sb("over", [128, E * MOST])
        place = sb("place", [128, E * MOST])
        n_tok = sb("n_tok", [128, E])
        n_blk = sb("n_blk", [128, E])
        blk_end = sb("blk_end", [128, E])
        base = sb("base", [128, E])
        slot_e = sb("slot_e", [128, MOST, E])
        slot_f = sb("slot_f", [128, MOST])
        slot = sb("slot", [128, N_TILES], i32)
        rT = sb("rT", [128, 2, RG * 128])
        past = sb("past", [1, NB, E])
        expert_f = sb("expert_f", [1, NB])
        expert = sb("expert", [1, NB], i32)
        xs = sb("xs", [128, 2, C])
        xT = sb("xT", [128, 2, 128])
        fcb = sb("fcb", [128, 2, HID])
        hT = sb("hT", [128, 2, KT, 128])
        ys = sb("ys", [128, 2, C])
        no_token = hT[:, :, :, :].rearrange("p v k c -> p (v k c)")[:, 0:ROW]
        xb = sb("xb", [128, 4, C])
        xnT = sb("xnT", [128, 2, 4 * 128])
        bq4s = sb("bq4s", [128, DENSE])
        qT = sb("qT", [128, 2, DENSE, 512])
        kT = sb("kT", [128, 2, 512])
        qkg = sb("qkg", [128, 2, 4, QKG])
        ks = sb("ks", [128, 2, SHIFTS, 4, LC])
        ks4 = sb("ks4", [128, 2, SHIFTS, 4, HEAD])
        prod = sb("prod", [128, SHIFTS, 4, LC])
        prod4 = sb("prod4", [128, SHIFTS, 4, HEAD])
        part = sb("part", [128, SHIFTS, 4, LC])
        part4 = sb("part4", [128, SHIFTS, 4, HEAD])
        sc = sb("sc", [128, 8, 4, LIGHT])
        scm = sb("scm", [128, 8 * 4 * LIGHT])
        lmax = sb("lmax", [128, 4 * LIGHT])
        pl = sb("pl", [128, 8 * 4 * LIGHT])
        pl4 = pl[:, :].rearrange("p (s t h) -> p s t h", s=8, t=4)
        osh = sb("osh", [128, 4, LC])
        o4 = sb("o4", [128, 4 * HEAD])
        nmax = sb("nmax", [128, 4, DENSE])
        PT = sb("PT", [128, 2, SLOTS, 128])
        v_side = sb("v_side", [128, 2, 3, (DENSE - 1) * HEAD])
        den = sb("den", [128, 2, 4, N_HEADS])
        den_side = sb("den_side", [128, 2, 4, DENSE])
        gmax = sb("gmax", [128, 4])
        gl = sb("gl", [128, 4, N_HEADS])
        ge = sb("ge", [128, 2, 4, N_HEADS])
        gsum = sb("gsum", [128, 4])
        dg = sb("dg", [128, 4, N_HEADS])
        rc = sb("rc", [128, 4, N_HEADS])
        fac = sb("fac", [128, 4, N_HEADS])
        gated = fcb[:, 0, :].rearrange("p (t c) -> p t c", t=4)
        gT = fcb[:, 1, :]

        rows_d = nc.dram_tensor("rows_d", [NB * 128, C], f32, kind="Internal")
        late_rows_d = nc.dram_tensor("late_rows_d", [NB * 128, ROW], f32, kind="Internal")
        y_d = nc.dram_tensor("y_d", [NB * 128, C], f32, kind="Internal")
        k_d = nc.dram_tensor("k_d", [PAD + B * T, LC], f32, kind="Internal")

        x_v = x_in.rearrange("b t c -> (b t) c").rearrange("(n p) c -> p n c", p=128)
        out_rows = out.rearrange("b t c -> (b t) c")

        x_in_s = [sem(f"x_loaded{n}") for n in range(len(LN1))]
        const_s = sem("constants_loaded")
        late_const_s = sem("masks_loaded")
        route_w_s = sem("router_weights_loaded")
        ffn_w_s = sem("expert_weights_loaded")
        att_w_s = sem("attention_weights_loaded")
        cleared_s = sem("buffers_cleared")
        zero_s = sem("dram_padding_zeroed")
        no_row_s = sem("row_without_token_ready")
        no_token_s = sem("rows_without_token_stored")
        xid_s = [sem(f"late_rows_loaded{n}") for n in range(3)]
        masks_s = sem("masks_cast")
        step_s = sem("vector_step")
        xres_s = sem("residual_updated")
        mean_s = sem("means_ready")
        cent_s = sem("rows_centred")
        sq_s = sem("squares_ready")
        var_s = sem("squares_summed")
        rstd_s = sem("spread_known")
        norm_s = sem("rows_normalised")
        rt_px_s = sem("route_rows_transposed")
        rt_T_s = sem("route_transposes_copied")
        logit_s = sem("logits_ready")
        hot_s = sem("expert_choice_ready")
        rank_s = sem("ranks_ready")
        slot_s = sem("slots_ready")
        scat_s = [sem(f"rows_scattered{n}") for n in range(2)]
        gath_s = [sem(f"outputs_gathered{n}") for n in range(B)]
        ld_s = sem("pair_loaded")
        st_s = [sem(f"block_stored{n}") for n in range(2)]
        px_s = sem("pair_transposed")
        xT_s = sem("pair_transpose_copied")
        h_s = sem("hidden_ready")
        r_s = sem("relu_ready")
        hT_s = sem("hidden_squared")
        py_s = sem("block_output_ready")
        y_s = sem("block_output_copied")
        bias_s = sem("output_bias_added")
        bq_s = sem("query_bias_scaled")
        xb_s = sem("batch_normalised")
        a_px_s = sem("batch_transposed")
        a_xT_s = sem("batch_transpose_copied")
        q_s = sem("dense_queries_ready")
        k_s = sem("dense_keys_ready")
        qkT_s = sem("dense_qk_copied")
        qkg_p_s = sem("qkg_ready")
        qkg_s = sem("qkg_biased")
        kw_s = sem("keys_written")
        ks_s = [sem(f"shifted_keys_loaded{n}") for n in range(2)]
        v_side_s = [sem(f"side_values_loaded{n}") for n in range(2)]
        s_s = sem("dense_scores_ready")
        nmax_s = sem("dense_max_ready")
        p_s = sem("dense_probs_ready")
        pt_s = sem("dense_probs_transposed")
        ptc_s = sem("dense_probs_copied")
        pv_s = sem("dense_outputs_ready")
        lprod_s = sem("light_products_ready")
        lsc_s = sem("light_scores_ready")
        lp_s = sem("light_probs_ready")
        lpart_s = sem("light_parts_ready")
        gl_s = sem("gate_logits_ready")
        ge_s = sem("gates_ready")
        gated_s = sem("gated_ready")
        gp_s = sem("gated_transposed")
        gT_s = sem("gated_copied")
        proj_s = sem("projection_ready")
        att_s = sem("attention_added")
        out_s = sem("output_stored")

        FILL = 8
        EARLY_OUT = 6
        LATE = ((0, 8), (8, NBS[1][0]), (NBS[1][0], NB))

        def placed(f, h):
            return sum(SEG_TILES[g][h] for g in range(f + 1))

        def probs_after(i, n):
            return 16 * i + 4 + 2 * n

        def batch(i):
            return slice(4 * i, 4 * i + 4)

        def len_of(tiles):
            return tiles.stop - tiles.start

        def runs(lo, hi, alone):
            cuts = sorted({lo, hi, *(c for a in alone for c in (a, a + 1) if lo <= c <= hi)})
            return list(zip(cuts, cuts[1:]))

        def ahead(i, n, k):
            i, n = i + (n + k) // UNITS, (n + k) % UNITS
            return (i, n) if i < B else None

        def unit(n):
            if n == 0:
                return 0, [(h, h * 128, 128) for h in range(DENSE)]
            t, k = (n + 1) // 2, (n - 1) % 2
            return t, [(h, SCORE_AT[h][1], 128 + PREV[h]) for h in (2 * k, 2 * k + 1)]

        def slots(n):
            return range(1, DENSE + 1) if n == 0 else range(3) if n % 2 else range(3, SLOTS)

        block = ctx.enter_context(nc.Block())

        def normalise_batch(eng, i):
            eng.wait_ge(rstd_s, len(SEG[0]) + 1 + [4 * i < tiles.stop for tiles in LN2].index(True))
            if i:
                eng.wait_ge(a_px_s, i)
            eng.tensor_tensor(xb[:, :, :], xn[:, ds(i * 4, 4), :],
                              rstd[:, ds(i * 4, 4)].unsqueeze(2).to_broadcast([128, 4, C]), ALU.mult).then_inc(xb_s, 1)

        def light_products(eng, i, u):
            lq = qkg[:, u, :, LQ:LQ + LC]
            eng.wait_ge(ks_s[u], (i // 2 + 1) * 32 * SHIFTS)
            if i:
                eng.wait_ge(lsc_s, i)
            eng.tensor_tensor(prod4[:, :, :, :], ks4[:, u, :, :, :],
                              lq[:, :, 0:HEAD].unsqueeze(1).to_broadcast([128, SHIFTS, 4, HEAD]), ALU.mult)
            eng.tensor_tensor(prod[:, :, :, :], ks[:, u, :, :, :],
                              lq.unsqueeze(1).to_broadcast([128, SHIFTS, 4, LC]), ALU.mult).then_inc(lprod_s, 1)

        def light_parts(eng, i, u):
            eng.wait_ge(lp_s, i + 1)
            eng.tensor_tensor(part4[:, :, :, :].rearrange("p s t d -> p (s t) d"),
                              ks4[:, u, :, :, :].rearrange("p s t d -> p (s t) d"),
                              pl4[:, 0:SHIFTS, :, 0].rearrange("p s t -> p (s t)").unsqueeze(2).to_broadcast(
                                  [128, SHIFTS * 4, HEAD]), ALU.mult)
            eng.tensor_tensor(part[:, :, :, :].rearrange("p s t (h d) -> p (s t h) d", d=HEAD),
                              ks[:, u, :, :, :].rearrange("p s t (h d) -> p (s t h) d", d=HEAD),
                              pl4[:, SHIFTS:, :, :].rearrange("p s t h -> p (s t h)").unsqueeze(2).to_broadcast(
                                  [128, SHIFTS * 4 * LIGHT, HEAD]), ALU.mult).then_inc(lpart_s, 1)

        def normalise(eng, f, r, tiles):
            eng.wait_ge(rstd_s, r)
            eng.wait_ge(rt_px_s, GROUPS * f + tiles.stop // RG)
            eng.tensor_tensor(xn[:, tiles, :], xn[:, tiles, :],
                              rstd[:, tiles].unsqueeze(2).to_broadcast([128, len_of(tiles), C]), ALU.mult).then_inc(norm_s, 1)

        @block.sync
        def _(sp):
            for n, tiles in enumerate(LN1):
                sp.dma_start(x[:, tiles, :], x_v[:, tiles, :]).then_inc(x_in_s[n], 16)
                if n == 0:
                    sp.dma_start(cst[:, 0:SOON], consts[:, 0:SOON]).then_inc(const_s, 16)
                    sp.dma_start(wr[:, :], w_router).then_inc(route_w_s, 16)
            sp.dma_start(cst[:, SOON:], consts[:, SOON:]).then_inc(late_const_s, 16)
            sp.wait_ge(cleared_s, 1)
            for k in range(2):
                sp.dma_start(rows_d[k * NP * 128:(k + 1) * NP * 128, :].rearrange("(p n) c -> p n c", p=128),
                             yg[:, 0:NP, :]).then_inc(zero_s, 16)
            sp.dma_start(k_d[0:PAD, :], yg[0:PAD, 0, 0:LC]).then_inc(zero_s, 16)
            sp.dma_start(fc[:, :, :], w_fc.rearrange("e d h -> d e h")).then_inc(ffn_w_s, 16)
            sp.dma_start(wo[:, :, :, :].rearrange("p e k d -> p (e k) d"),
                         w_out.rearrange("e (k p) d -> p (e k) d", p=128)).then_inc(ffn_w_s, 16)
            for dst, src in ((wqkg, w_qkg), (wq4, w_q4), (wk4, w_k4), (bq4, b_q4), (bk4, b_k4), (wproj, w_proj)):
                sp.dma_start(dst[:, :], src).then_inc(att_w_s, 16)
            sp.dma_start(bqkg[:, :], b_qkg.to_broadcast([128, QKG])).then_inc(att_w_s, 16)
            sp.dma_start(bproj[:, :], b_proj.to_broadcast([128, C])).then_inc(att_w_s, 16)

            def load(f, j):
                src = late_rows_d[ds(j * 256, 256), 0:C] if f else rows_d[ds(j * 256, 256), :]
                sp.dma_start(xs[:, :, :], src.rearrange("(u p) c -> p u c", p=128)).then_inc(ld_s, 16)

            def load_late(f, k):
                if f:
                    a, b = LATE[k]
                    sp.dma_start(xid[:, a:b, :], late_rows_d[a * 128:b * 128, C:].rearrange("(n p) c -> p n c", p=128)
                                 ).then_inc(xid_s[k], 16)

            def store(f, j, v):
                if f:
                    return
                sp.wait_ge(y_s, 2 * j + v + 1)
                sp.dma_start(y_d[ds(j * 256 + v * 128, 128), :], ys[:, v, :]).then_inc(st_s[v], 16)

            def ffn(f):
                def step(j, first=False, last=False):
                    if not first:
                        store(f, j - 1, 1)
                    if not last:
                        sp.wait_ge(px_s, j + (NP * f + 2))
                        load(f, j + 2)
                    store(f, j, 0)

                sp.wait_ge(scat_s[0], 16 * placed(f, 0))
                load(f, 0)
                load_late(f, 0)
                sp.wait_ge(px_s, NP * f + 1)
                load(f, 1)
                load_late(f, 1)
                step(0, first=True)
                with sp.Fori(1, CROSS[f] - 2) as j:
                    step(j)
                sp.wait_ge(scat_s[1], 16 * placed(f, 1))
                load_late(f, 2)
                with sp.Fori(CROSS[f] - 2, NP - 2) as j:
                    step(j)
                step(NP - 2, last=True)
                step(NP - 1, last=True)
                store(f, NP - 1, 1)

            def keys(i, u):
                sp.wait_ge(qkg_s, 2 * i + 2)
                sp.dma_start(k_d[ds(i * T + PAD, T), :].rearrange("(t p) c -> p t c", p=128),
                             qkg[:, u, :, LK:LK + LC]).then_inc(kw_s, 16)
                sp.wait_ge(kw_s, i * 16 + 16)
                for s in range(SHIFTS):
                    sp.dma_start(ks[:, u, s, :, :],
                                 k_d[ds(i * T + (PAD + s + 1 - SHIFTS), T), :].rearrange("(t p) c -> p t c", p=128)
                                 ).then_inc(ks_s[u], 16)
                for s in range(SHIFTS):
                    sp.dma_start(ks4[:, u, s, :, :],
                                 k_d[ds(i * T + (PAD + s + 1 - 2 * SHIFTS), T), 0:HEAD].rearrange(
                                     "(t p) c -> p t c", p=128)).then_inc(ks_s[u], 16)
                for h in range(1, DENSE):
                    sp.dma_start(v_side[SIDE[h]:SIDE[h] + PREV[h], u, :, (h - 1) * HEAD:h * HEAD],
                                 qkg[128 - PREV[h]:128, u, 0:3, DK + h * HEAD:DK + (h + 1) * HEAD]
                                 ).then_inc(v_side_s[u], 16)

            ffn(0)
            sp.wait_ge(zero_s, 48)
            sp.wait_ge(no_row_s, 1)
            for i in range(B):
                keys(i, i % 2)
                a, b = i * FILL, min((i + 1) * FILL, NB)
                if a < b:
                    sp.dma_start(late_rows_d[a * 128:b * 128, :].rearrange("(p n) c -> p n c", p=128),
                                 no_token.unsqueeze(1).to_broadcast([128, b - a, ROW])).then_inc(no_token_s, 16)
            ffn(1)
            sp.wait_ge(out_s, 16 * NB)

        @block.gpsimd
        def _(pool):
            pool.memset(yg[:, 0:NP, :], 0.0).then_inc(cleared_s, 1)
            pool.memset(ones[:, :], 1.0).then_inc(cleared_s, 1)
            pool.memset(P[:, :, :, :], 0.0).then_inc(cleared_s, 1)
            pool.memset(v_side[:, :, :, :], 0.0).then_inc(cleared_s, 1)
            pool.memset(den_side[:, :, :, :], 0.0).then_inc(cleared_s, 1)
            pool.memset(sc[:, :, :, :], -BIG).then_inc(cleared_s, 1)


            def scatter(f, h, tiles, steps):
                pool.wait_ge(norm_s, steps)
                pool.wait_ge(slot_s, 2 * f + h + 1)
                for t in range(tiles.start, tiles.stop):
                    pool.indirect_dma_start(
                        out=(late_rows_d if f else rows_d)[:, :],
                        out_offset=bass.IndirectOffsetOnAxis(ap=slot[:, t:t + 1].bitcast(u32), axis=0),
                        in_=rows[:, t, :] if f else xn[:, t, :], in_offset=None).then_inc(scat_s[h], 16)

            def put_out(blocks):
                for b in blocks:
                    pool.wait_ge(y_s, 2 * NP + b + 1)
                    pool.indirect_dma_start(
                        out=out_rows, out_offset=bass.IndirectOffsetOnAxis(ap=xid[:, b, C:C + 1].bitcast(u32), axis=0),
                        in_=xid[:, b, 0:C], in_offset=None, bounds_check=B * T - 1, oob_is_err=False).then_inc(out_s, 16)

            def gather(h):
                for v in range(2):
                    pool.wait_ge(st_s[v], 16 * (CROSS[0] + 1 if h == 0 else NP))
                for t in range(SEG[0][h].start, SEG[0][h].stop):
                    pool.indirect_dma_start(
                        out=yg[:, t, :], out_offset=None, in_=y_d[0:(BLOCK0[0][h] + NBS[0][h]) * 128, :],
                        in_offset=bass.IndirectOffsetOnAxis(ap=slot[:, t:t + 1].bitcast(u32), axis=0)
                    ).then_inc(gath_s[t // 4], 16)

            def squares(n, tiles):
                pool.wait_ge(cent_s, n + 1)
                pool.wait_ge(var_s, n)
                pool.tensor_tensor(sq[:, 0:len_of(tiles), :], xn[:, tiles, :], xn[:, tiles, :], ALU.mult).then_inc(sq_s, 1)

            def centre(tiles):
                pool.wait_ge(mean_s, 1)
                pool.tensor_tensor(xn[:, tiles, :], x[:, tiles, :],
                                   rowsum[:, tiles].unsqueeze(2).to_broadcast([128, len_of(tiles), C]), ALU.add
                                   ).then_inc(cent_s, 1)

            def add_output_bias(n, tiles):
                pool.wait_ge(att_w_s, 16 * 8)
                pool.wait_ge(cent_s, n + 1)
                pool.tensor_tensor(x[:, tiles, :], x[:, tiles, :],
                                   bproj[:, :].unsqueeze(1).to_broadcast([128, len_of(tiles), C]), ALU.add).then_inc(bias_s, 1)

            def window(i):
                if i > 0:
                    light_products(pool, i, i % 2)
                if i + 2 < B:
                    normalise_batch(pool, i + 2)
                if i == 1:
                    centre(LN2[2])
                    squares(6, LN2[2])
                if 3 <= i < 7:
                    normalise(pool, 1, len(SEG[0]) + len(LN2) + 1 + i - 3, batch(i - 3))
                if i == 2:
                    add_output_bias(6, slice(LN2[1].start, N_TILES))
                if i + 1 < B:
                    light_parts(pool, i, i % 2)

            pool.wait_ge(zero_s, 48)
            scatter(0, 0, SEG[0][0], 1)
            scatter(0, 1, SEG[0][1], 2)
            gather(0)
            squares(4, LN2[0])
            normalise_batch(pool, 0)
            gather(1)
            add_output_bias(4, LN2[0])
            for i in range(B):
                window(i)
            pool.wait_ge(no_token_s, 16 * -(-NB // FILL))
            scatter(1, 0, slice(0, 16), 6)
            scatter(1, 0, batch(4), 7)
            put_out(range(0, EARLY_OUT))
            normalise(pool, 1, len(SEG[0]) + len(LN2) + 6, SEG[1][1])
            scatter(1, 1, SEG[1][1], 8)
            put_out(range(EARLY_OUT, NB))

        @block.scalar
        def _(act):
            act.preload_act_table(ACT.Exp)

            def squares(n, tiles, at=0):
                act.wait_ge(cent_s, n + 1)
                if at == 0 and n:
                    act.wait_ge(var_s, n)
                act.activation(sq[:, at:at + len_of(tiles), :], xn[:, tiles, :], ACT.Square).then_inc(sq_s, 1)

            def square_sums(n, tiles):
                act.wait_ge(cent_s, n + 1)
                act.wait_ge(var_s, n)
                for t in range(tiles.start, tiles.stop):
                    ins = act.activation(sq[:, t - tiles.start, :], xn[:, t, :], ACT.Square, accum_out=var[:, t:t + 1])
                ins.then_inc(var_s, 1)

            def route_copy(f, g, banks):
                m = GROUPS * f + g
                act.wait_ge(rt_px_s, m + 1)
                if m >= 2:
                    act.wait_ge(logit_s, m - 1)
                act.activation(rT[:, m % 2, :], bank[banks[g % 2]][:, 0:RG * 128], ACT.Copy).then_inc(rt_T_s, 1)

            def copy_rows(f, j, v):
                if v == 0:
                    act.wait_ge(px_s, j + (NP * f + 1))
                act.activation(xT[:, v, :], bank[5][:, v * 128:(v + 1) * 128], ACT.Copy).then_inc(xT_s, 1)

            its_expert = [act.alloc_register(f"expert_of_block{v}") for v in range(2)]

            def load_expert(j, v):
                act.reg_load(its_expert[v], expert[0:1, ds(2 * j + v, 1)])

            def copy_weights(v):
                e = act.snap(its_expert[v], min_val=0, max_val=E - 1)
                act.activation(fcb[:, v, :], fc[:, ds(e, 1), :].rearrange("p e h -> p (e h)"), ACT.Copy)

            def squares_of(f, j, v):
                act.wait_ge(r_s, 2 * j + (2 * NP * f + v + 1))
                block_h = hT[:, v, :, :].rearrange("p k c -> p (k c)")
                act.activation(block_h, block_h, ACT.Square).then_inc(hT_s, 1)

            def ffn_step(f, j, left=2):
                if left == 0:
                    squares_of(f, j, 0)
                    squares_of(f, j, 1)
                    return
                act.wait_ge(h_s, 2 * j + (2 * NP * f + 1))
                copy_weights(0)
                squares_of(f, j, 0)
                load_expert(j + 1, 1)
                copy_rows(f, j + 1, 0)
                act.wait_ge(h_s, 2 * j + (2 * NP * f + 2))
                copy_weights(1)
                copy_rows(f, j + 1, 1)
                if left > 1:
                    load_expert(j + 2, 0)
                squares_of(f, j, 1)

            def ffn(f, work, before=()):
                for v in range(2):
                    load_expert(0, v)
                    if f and v:
                        act.wait_ge(proj_s, B)
                    copy_weights(v)
                load_expert(1, 0)
                for w in before:
                    w()
                for v in range(2):
                    copy_rows(f, 0, v)
                for lo, hi in runs(0, NP - 2, work):
                    for w in work.get(lo, ()):
                        w()
                    if hi > lo + 1:
                        with act.Fori(lo, hi) as j:
                            ffn_step(f, j)
                    else:
                        ffn_step(f, lo)
                ffn_step(f, NP - 2, left=1)
                ffn_step(f, NP - 1, left=0)

            def copy_batch(i):
                act.wait_ge(a_px_s, i + 1)
                act.activation(xnT[:, i % 2, :], bank[6][:, :], ACT.Copy).then_inc(a_xT_s, 1)

            def copy_queries(i, heads):
                act.wait_ge(q_s, i + 1)
                for h in heads:
                    act.activation(qT[:, i % 2, h, :], bank[7][:, :], ACT.Identity, bias=bq4s[:, h:h + 1],
                                   scale=const("head_scale")[:, h:h + 1]).then_inc(qkT_s, 1)

            def copy_keys(i):
                act.wait_ge(k_s, i + 1)
                act.activation(kT[:, i % 2, :], bank[6][:, :], ACT.Identity, bias=bk4[:, 0:1]).then_inc(qkT_s, 1)

            def dense_probs(i, n):
                act.wait_ge(nmax_s, UNITS * i + n + 1)
                if n == 1 and i:
                    act.wait_ge(pt_s, UNITS * i)
                t, heads = unit(n)
                rows = P[:, t % 2, :, :].rearrange("p s k -> p (s k)")
                for h, a0, w in heads:
                    s, to = bank[(n + i) % 2], 128 * (h + 1)
                    if 0 < h and 128 < w:
                        side = 128 * (SLOTS - 1) + SIDE[h]
                        act.activation(rows[:, side:side + w - 128], s[:, a0:a0 + w - 128], ACT.Exp,
                                       bias=nmax[:, t, h:h + 1], accum_out=den_side[:, i % 2, t, h:h + 1])
                        a0, w = a0 + w - 128, 128
                    act.activation(rows[:, to + 128 - w:to + 128], s[:, a0:a0 + w], ACT.Exp,
                                   bias=nmax[:, t, h:h + 1], accum_out=den[:, i % 2, t, h:h + 1]).then_inc(p_s, 1)

            def copy_probs(i, n):
                t = (n + 1) // 2
                act.wait_ge(pt_s, UNITS * i + n + 1)
                if 4 * i + t > 1:
                    act.wait_ge(pv_s, 4 * i + t - 1)
                k = slots(n)
                act.activation(PT[:, t % 2, k.start:k.stop, :].rearrange("p s q -> p (s q)"),
                               bank[3][:, 0:128 * len(k)], ACT.Copy).then_inc(ptc_s, 1)

            def light_probs(i):
                act.wait_ge(lsc_s, i + 1)
                act.activation(pl[:, :], scm[:, :], ACT.Exp, scale=SCALE).then_inc(lp_s, 1)

            def gates(i):
                act.wait_ge(gl_s, i + 1)
                act.activation(ge[:, i % 2, :, :], gl[:, :, :], ACT.Exp).then_inc(ge_s, 1)

            def copy_gated(i):
                act.wait_ge(gp_s, i + 1)
                act.activation(gT, bank[6][:, :], ACT.Copy).then_inc(gT_s, 1)

            def slot_of(i, n):
                nxt = ahead(i, n, 1)
                if nxt:
                    dense_probs(*nxt)
                copy_probs(i, n)
                if i + 1 < B:
                    if n == 0:
                        copy_batch(i + 1)
                    if n in (1, 2):
                        copy_queries(i + 1, (2 * n - 2, 2 * n - 1))
                    if n == 3:
                        copy_keys(i + 1)
                    if n == 6:
                        gates(i + 1)
                if n == (5 if i + 1 < B else 4):
                    light_probs(i)
                if n == 4 and i:
                    copy_gated(i - 1)
                if (i, n) == (0, 4):
                    squares(5, LN2[1])
                if i >= 2 and n == (1 if 2 < i < B - 1 else 3 if i == 2 else 5):
                    (squares if i + 1 < B else square_sums)(7 + i - 2, batch(i - 2))
                at = 5 if i + 1 == B else 1
                if i >= 2 and n in (at, at + 1):
                    route_copy(1, 2 * (i - 2) + n - at, (2, 2))

            squares(0, LN1[0])
            squares(1, LN1[1], at=LN1[0].stop)
            for g in range(GROUPS):
                for n in (2, 3):
                    if RG * g == LN1[n].start:
                        squares(n, LN1[n])
                route_copy(0, g, (6, 7))
            act.wait_ge(late_const_s, 16)
            act.activation(identb[:, :], ident, ACT.Copy).then_inc(masks_s, 1)
            a, b_ = CONST_AT["mask_first"][0], CONST_AT["mask_rest"][1]
            act.activation(maskb[:, :], cst[:, a:b_], ACT.Copy).then_inc(masks_s, 1)
            act.wait_ge(slot_s, 1)
            act.wait_ge(ffn_w_s, 32)
            ffn(0, {CROSS[0] - 2: [lambda: act.wait_ge(slot_s, 2)]})
            act.wait_ge(att_w_s, 16 * 8)
            act.activation(bq4s[:, :], bq4[:, :], ACT.Copy, scale=SCALE).then_inc(bq_s, 1)
            copy_batch(0)
            act.wait_ge(bq_s, 1)
            copy_queries(0, range(DENSE))
            copy_keys(0)
            gates(0)
            dense_probs(0, 0)
            for i in range(B):
                for n in range(UNITS):
                    slot_of(i, n)
            copy_gated(B - 1)
            route_copy(1, 12, (2, 4))
            route_copy(1, 13, (2, 4))
            act.wait_ge(slot_s, 3)
            ffn(1, {0: [lambda: square_sums(13, batch(B - 2))], 1: [lambda: square_sums(14, batch(B - 1))],
                    CROSS[1] - 2: [lambda: act.wait_ge(slot_s, 4)]},
                before=[lambda: route_copy(1, 14, (2, 4)), lambda: route_copy(1, 15, (2, 4))])

        @block.vector
        def _(dve):
            steps = [0]

            def step(ins):
                steps[0] += 1
                ins.then_inc(step_s, 1)
                dve.wait_ge(step_s, steps[0])

            def row_sums(tiles):
                step(nc.vector.tensor_reduce(rowsum[:, tiles], x[:, tiles, :], AX.X, ALU.add))

            def means(tiles):
                nc.vector.tensor_scalar(rowsum[:, tiles], rowsum[:, tiles], -1.0 / C, None, ALU.mult).then_inc(mean_s, 1)

            def over_c(a, tiles):
                return a[:, tiles].unsqueeze(2).to_broadcast([128, tiles.stop - tiles.start, C])

            def centre(tiles, more=False):
                ins = nc.vector.scalar_tensor_tensor(xn[:, tiles, :], over_c(rowsum, tiles), -1.0 / C,
                                                     x[:, tiles, :], ALU.mult, ALU.add)
                if not more:
                    ins.then_inc(cent_s, 1)

            def sum_squares(n, tiles, at, more=False):
                dve.wait_ge(sq_s, n + 1)
                ins = nc.vector.tensor_reduce(var[:, tiles], sq[:, at:at + len_of(tiles), :], AX.X, ALU.add)
                if not more:
                    ins.then_inc(var_s, 1)

            def variance(n, tiles):
                sum_squares(n, tiles, 0)

            def root_guess(n, tiles):
                dve.wait_ge(var_s, n + 1)
                step(nc.vector.tensor_scalar(var[:, tiles], var[:, tiles], 1.0 / C, EPS, ALU.mult, ALU.add))
                step(nc.vector.tensor_scalar(rstd[:, tiles].bitcast(i32), var[:, tiles].bitcast(i32),
                                             -0.5, float(0x5f3759df), ALU.mult, ALU.add))

            def root_step(tiles, last=False):
                near = newton[:, 0:len_of(tiles)]
                step(nc.vector.tensor_tensor(near, rstd[:, tiles], rstd[:, tiles], ALU.mult))
                step(nc.vector.scalar_tensor_tensor(near, near, -0.5, var[:, tiles], ALU.mult, ALU.mult))
                root = nc.vector.scalar_tensor_tensor(rstd[:, tiles], near, 1.5, rstd[:, tiles], ALU.add, ALU.mult)
                if last:
                    root.then_inc(rstd_s, 1)
                else:
                    step(root)

            def spread(n, tiles):
                root_guess(n, tiles)
                for k in range(3):
                    root_step(tiles, last=k == 2)

            def choose(f, h, b):
                k = SEG_TILES[f][h]
                logits = bank[b][:, 512 - k * E:].rearrange("p (t e) -> p t e", e=E)

                def along(ap):
                    return ap.unsqueeze(2).to_broadcast([128, k, E])

                dve.wait_ge(logit_s, GROUPS * f + SEG[f][h].stop // RG)
                step(nc.vector.tensor_reduce(top[:, 0:k], logits, AX.X, ALU.max))
                step(nc.vector.tensor_tensor(tied[:, 0:k, :], logits, along(top[:, 0:k]), ALU.is_equal))
                step(nc.vector.tensor_tensor(tied[:, 0:k, :], tied[:, 0:k, :],
                                             const("first_of_ties").unsqueeze(1).to_broadcast([128, k, E]), ALU.mult))
                step(nc.vector.tensor_reduce(top2[:, 0:k], tied[:, 0:k, :], AX.X, ALU.max))
                nc.vector.tensor_tensor(hot[:, 0:k, :], tied[:, 0:k, :], along(top2[:, 0:k]),
                                        ALU.is_equal).then_inc(hot_s, 1)

            def by_expert(a, k):
                return a[:, 0:E * k].rearrange("p (e t) -> p e t", e=E)

            def count_blocks(f, h, b):
                k = SEG_TILES[f][h]
                counts = bank[b][:, k * E:2 * k * E].rearrange("p (t e) -> p e t", e=E)
                dve.wait_ge(rank_s, 2 * f + h + 1)
                step(nc.vector.tensor_copy(by_expert(cnt, k), counts))
                step(nc.vector.tensor_tensor_scan(upto[:, 0:E * k], ones[:, 0:E * k], cnt[:, 0:E * k], 0.0, ALU.mult, ALU.add))
                step(nc.vector.tensor_tensor(before[:, 0:E * k], upto[:, 0:E * k], cnt[:, 0:E * k], ALU.subtract))
                step(nc.vector.tensor_tensor(n_tok[:, :], by_expert(upto, k)[:, :, k - 1], by_expert(before, k)[:, :, 0],
                                             ALU.subtract))
                step(nc.vector.tensor_tensor(by_expert(over, k), n_tok[:, :].unsqueeze(2).to_broadcast([128, E, k]),
                                             const("full_blocks")[:, 0:k].unsqueeze(1).to_broadcast([128, E, k]), ALU.is_gt))
                step(nc.vector.tensor_reduce(n_blk[:, :], by_expert(over, k), AX.X, ALU.add))
                step(nc.vector.tensor_tensor_scan(blk_end[:, :], ones[:, 0:E], n_blk[:, :], 0.0, ALU.mult, ALU.add))

            def place_blocks(f, h):
                k, blocks, b0 = SEG_TILES[f][h], NBS[f][h], BLOCK0[f][h]
                step(nc.vector.tensor_tensor(base[:, :], blk_end[:, :], n_blk[:, :], ALU.subtract))
                step(nc.vector.scalar_tensor_tensor(base[:, :], base[:, :], 128.0, by_expert(before, k)[:, :, 0],
                                                    ALU.mult, ALU.subtract))
                step(nc.vector.tensor_tensor(past[:, 0:blocks, :],
                                             const("block_no")[0:1, 0:blocks].unsqueeze(2).to_broadcast([1, blocks, E]),
                                             blk_end[0:1, :].unsqueeze(1).to_broadcast([1, blocks, E]), ALU.is_ge))
                step(nc.vector.tensor_reduce(expert_f[:, 0:blocks], past[:, 0:blocks, :], AX.X, ALU.add))
                step(nc.vector.tensor_scalar(expert[:, b0:b0 + blocks], expert_f[:, 0:blocks], float(E - 1), None, ALU.min))

            def place_tokens(f, h, b):
                k = SEG_TILES[f][h]
                ranks = bank[b][:, 0:k * E].rearrange("p (t e) -> p t e", e=E)
                step(nc.vector.tensor_tensor(by_expert(place, k), by_expert(before, k),
                                             base[:, :].unsqueeze(2).to_broadcast([128, E, k]), ALU.add))
                step(nc.vector.tensor_tensor(slot_e[:, 0:k, :], by_expert(place, k).rearrange("p e t -> p t e"), ranks,
                                             ALU.add))
                step(nc.vector.tensor_tensor(slot_e[:, 0:k, :], slot_e[:, 0:k, :], hot[:, 0:k, :], ALU.mult))
                step(nc.vector.tensor_reduce(slot_f[:, 0:k], slot_e[:, 0:k, :], AX.X, ALU.add))
                nc.vector.tensor_scalar(slot[:, SEG[f][h]], slot_f[:, 0:k], float(BLOCK0[f][h] * 128), None,
                                        ALU.add).then_inc(slot_s, 1)

            def relu(f, j, v):
                dve.wait_ge(h_s, 2 * j + (2 * NP * f + v + 1))
                nc.vector.tensor_scalar(hT[:, v, :, :].rearrange("p k c -> p (k c)"), bank[v][:, :], 0.0, None,
                                        ALU.max).then_inc(r_s, 1)

            def copy_out(f, j, v, fresh=False):
                dve.wait_ge(py_s, 2 * j + (2 * NP * f + v + 1))
                made = bank[OUT_BANK[f] + v][:, 0:128]
                if f:
                    rest = xid[:, ds(2 * j + v, 1), 0:C]
                    nc.vector.scalar_tensor_tensor(rest, made.unsqueeze(1), 0.5, rest, ALU.mult, ALU.add).then_inc(y_s, 1)
                    return
                if not fresh:
                    dve.wait_ge(st_s[v], j * 16)
                nc.vector.tensor_copy(ys[:, v, :], made).then_inc(y_s, 1)

            def ffn_step(f, j, first=False, second=False, between=()):
                relu(f, j, 0)
                if not first:
                    copy_out(f, j - 1, 1, fresh=second and f == 0)
                for w in between:
                    w()
                relu(f, j, 1)
                copy_out(f, j, 0, fresh=first and f == 0)

            def ffn(f, work):
                for lo, hi in runs(0, NP, {0, 1, *work}):
                    if hi > lo + 1:
                        with dve.Fori(lo, hi) as j:
                            ffn_step(f, j)
                    else:
                        between, after = work.get(lo, ((), ()))
                        ffn_step(f, lo, lo == 0, lo == 1, between)
                        for w in after:
                            w()
                copy_out(f, NP - 1, 1)

            def residual(tiles, n):
                for g in range(tiles.start // 4, tiles.stop // 4):
                    dve.wait_ge(gath_s[g], 64)
                nc.vector.scalar_tensor_tensor(x[:, tiles, :], yg[:, tiles, :], 0.5, x[:, tiles, :],
                                               ALU.mult, ALU.add).then_inc(xres_s, 1)
                dve.wait_ge(xres_s, n)

            def add_bias(i, k):
                dve.wait_ge(qkg_p_s, 2 * i + k + 1)
                nc.vector.tensor_tensor(qkg[:, i % 2, 2 * k:2 * k + 2, :],
                                        bank[5][:, 0:2 * QKG].rearrange("p (t c) -> p t c", t=2),
                                        bqkg[:, :].unsqueeze(1).to_broadcast([128, 2, QKG]), ALU.add).then_inc(qkg_s, 1)

            def dense_max(i, n):
                dve.wait_ge(s_s, UNITS * i + n + 1)
                t, heads = unit(n)
                s = bank[(n + i) % 2]
                if n == 0:
                    mx = nc.vector.tensor_reduce(nmax[:, 0, :], s[:, :].rearrange("p (h k) -> p h k", h=DENSE),
                                                 AX.X, ALU.max, negate=True)
                else:
                    for h, a0, w in heads:
                        mx = nc.vector.tensor_reduce(nmax[:, t, h:h + 1], s[:, a0:a0 + w], AX.X, ALU.max, negate=True)
                mx.then_inc(nmax_s, 1)

            def light_sums(i):
                dve.wait_ge(lprod_s, i + 1)
                nc.vector.tensor_reduce(sc[:, 0:SHIFTS, :, 0].rearrange("p s t -> p (s t)"),
                                        prod4[:, :, :, :].rearrange("p s t d -> p (s t) d"), AX.X, ALU.add)
                step(nc.vector.tensor_reduce(sc[:, SHIFTS:, :, :].rearrange("p s t h -> p (s t) h"),
                                             prod[:, :, :, :].rearrange("p s t (h d) -> p (s t) h d", d=HEAD),
                                             AX.X, ALU.add))
                step(nc.vector.tensor_tensor(sc[:, :, 0, :], sc[:, :, 0, :],
                                             const("light_mask").rearrange("p (s h) -> p s h", s=8), ALU.add))

            def light_scores(i):
                scm_s = scm[:, :].rearrange("p (s a) -> p s a", s=8)
                sc_s = sc[:, :, :, :].rearrange("p s t h -> p s (t h)")
                step(nc.vector.tensor_reduce(lmax[:, :], sc_s.rearrange("p s a -> p a s"), AX.X, ALU.max))
                nc.vector.tensor_tensor(scm_s, sc_s, lmax[:, :].unsqueeze(1).to_broadcast([128, 8, 4 * LIGHT]),
                                        ALU.subtract).then_inc(lsc_s, 1)

            def gate_logits(i):
                g = qkg[:, i % 2, :, GL:]
                dve.wait_ge(qkg_s, 2 * i + 2)
                if i:
                    dve.wait_ge(ge_s, i)
                step(nc.vector.tensor_reduce(gmax[:, :], g, AX.X, ALU.max))
                nc.vector.tensor_tensor(gl[:, :, :], g, gmax[:, :].unsqueeze(2).to_broadcast([128, 4, N_HEADS]),
                                        ALU.subtract).then_inc(gl_s, 1)

            def over_d(a):
                return a.unsqueeze(a.ndim).to_broadcast(list(a.shape) + [HEAD])

            def light_outputs(i):
                dve.wait_ge(lpart_s, i + 1)
                nc.vector.tensor_reduce(o4[:, :], part4[:, :, :, :].rearrange("p s t d -> p (t d) s"), AX.X, ALU.add)
                nc.vector.tensor_reduce(den[:, i % 2, :, DENSE:], pl4.rearrange("p s t h -> p t h s"), AX.X, ALU.add)
                step(nc.vector.tensor_reduce(osh[:, :, :].rearrange("p t c -> p (t c)"),
                                             part[:, :, :, :].rearrange("p s t c -> p (t c) s"), AX.X, ALU.add))
                step(nc.vector.tensor_tensor(osh[:, :, 0:HEAD], osh[:, :, 0:HEAD],
                                             o4[:, :].rearrange("p (t d) -> p t d", d=HEAD), ALU.add))

            def gate(i):
                u = i % 2
                dve.wait_ge(ge_s, i + 1)
                step(nc.vector.tensor_reduce(gsum[:, :], ge[:, u, :, :], AX.X, ALU.add))
                dve.wait_ge(p_s, probs_after(i, UNITS - 1))
                step(nc.vector.tensor_tensor(den[:, u, :, 0:DENSE], den[:, u, :, 0:DENSE], den_side[:, u, :, :], ALU.add))
                step(nc.vector.tensor_tensor(dg[:, :, :], den[:, u, :, :],
                                             gsum[:, :].unsqueeze(2).to_broadcast([128, 4, N_HEADS]), ALU.mult))
                step(nc.vector.reciprocal(rc[:, :, :], dg[:, :, :]))
                step(nc.vector.tensor_tensor(fac[:, :, :], ge[:, u, :, :], rc[:, :, :], ALU.mult))
                if i:
                    dve.wait_ge(gp_s, i)
                nc.vector.tensor_tensor(gated[:, :, DENSE * HEAD:].rearrange("p t (h d) -> p t h d", d=HEAD),
                                        osh[:, :, :].rearrange("p t (h d) -> p t h d", d=HEAD),
                                        over_d(fac[:, :, DENSE:]), ALU.mult)
                dve.wait_ge(pv_s, 4 * i + 4)
                nc.vector.tensor_tensor(gated[:, :, 0:DENSE * HEAD].rearrange("p t (h d) -> p t h d", d=HEAD),
                                        bank[4][:, 0:4 * DENSE * HEAD].rearrange("p (t h d) -> p t h d", t=4, d=HEAD),
                                        over_d(fac[:, :, 0:DENSE]), ALU.mult).then_inc(gated_s, 1)

            def attended(i):
                dve.wait_ge(proj_s, i + 1)
                dve.wait_ge(bias_s, 1 if i < LN2[0].stop // 4 else 2)
                nc.vector.tensor_tensor(x[:, ds(i * 4, 4), :], bank[7][:, :].rearrange("p (t c) -> p t c", t=4),
                                        x[:, ds(i * 4, 4), :], ALU.add).then_inc(att_s, 1)

            def half_attended(i):
                dve.wait_ge(att_s, i)

            besides = {
                (0, 2): lambda: light_products(nc.vector, 0, 0),
                (0, 0): lambda: residual(LN2[1], 4), (0, 1): lambda: row_sums(LN2[1]), (0, 3): lambda: centre(LN2[1]),
                (0, 5): lambda: variance(5, LN2[1]), (0, 6): lambda: spread(5, LN2[1]),
                (1, 1): lambda: residual(LN2[2], 5), (1, 2): lambda: (row_sums(LN2[2]), means(LN2[2])),
                (2, 1): lambda: variance(6, LN2[2]), (2, 4): lambda: spread(6, LN2[2]),
                (6, 4): lambda: choose(1, 0, 2),
                (6, 6): lambda: (count_blocks(1, 0, 2), place_blocks(1, 0)),
                (7, 1): lambda: place_tokens(1, 0, 2),
                (B - 1, 5): lambda: (light_parts(nc.vector, B - 1, (B - 1) % 2), light_outputs(B - 1)),
            }

            def slot_of(i, n):
                nxt = ahead(i, n, 2)
                if nxt:
                    dense_max(*nxt)
                if i >= 2 and n == (0 if i + 1 < B else 4):
                    half_attended(i - 1)
                    row_sums(batch(i - 2))
                    if i == 2:
                        dve.wait_ge(cent_s, len(LN1) + len(LN2))
                    centre(batch(i - 2))
                if i:
                    if n == 0:
                        light_outputs(i - 1)
                    if n == 1:
                        gate(i - 1)
                    if n == 6:
                        attended(i - 1)
                early = i + 1 == B
                if n == 3 - early:
                    light_sums(i)
                if i + 1 < B:
                    if n in (2, 4):
                        add_bias(i + 1, n // 2 - 1)
                    if n == 5:
                        gate_logits(i + 1)
                if n == 4 - early:
                    light_scores(i)
                if i >= 2:
                    if n == (4 if i == 2 else 2) and i + 1 < B:
                        variance(7 + i - 2, batch(i - 2))
                    if n == (6 if i == 2 else 5) and i < 6:
                        spread(7 + i - 2, batch(i - 2))
                if (i, n) in besides:
                    besides[i, n]()

            dve.wait_ge(const_s, 16)
            dve.wait_ge(cleared_s, 6)
            dve.wait_ge(x_in_s[0], 16)
            row_sums(LN1[0])
            centre(LN1[0])
            dve.wait_ge(x_in_s[1], 16)
            row_sums(LN1[1])
            centre(LN1[1])
            dve.wait_ge(x_in_s[2], 16)
            row_sums(LN1[2])
            centre(LN1[2])
            sum_squares(0, LN1[0], 0)
            sum_squares(1, LN1[1], LN1[0].stop)
            spread(1, SEG[0][0])
            choose(0, 0, 4)
            dve.wait_ge(x_in_s[3], 16)
            row_sums(LN1[3])
            centre(LN1[3])
            normalise(nc.vector, 0, 1, SEG[0][0])
            count_blocks(0, 0, 4)
            place_blocks(0, 0)
            place_tokens(0, 0, 4)
            variance(2, LN1[2])
            variance(3, LN1[3])
            spread(3, SEG[0][1])
            choose(0, 1, 3)
            normalise(nc.vector, 0, 2, SEG[0][1])
            count_blocks(0, 1, 3)
            place_blocks(0, 1)
            place_tokens(0, 1, 3)
            def add_early(i):
                return lambda: residual(batch(i), i + 1)

            def sum_early(i):
                return lambda: row_sums(batch(i))

            def centre_early(i):
                return lambda: centre(batch(i), more=i < 2)

            def squares_early(i):
                return lambda: sum_squares(4, batch(i), 4 * i, more=i < 2)

            def root_early(last=False):
                return lambda: root_step(LN2[0], last)

            ffn(0, {NP - 8: ([add_early(0)], [add_early(1)]),
                    NP - 7: ([add_early(2)], [sum_early(0)]),
                    NP - 6: ([sum_early(1)], [sum_early(2)]),
                    NP - 5: ([centre_early(0)], [centre_early(1)]),
                    NP - 4: ([centre_early(2)], ()),
                    NP - 3: ((), [squares_early(0)]),
                    NP - 2: ([squares_early(1)], [squares_early(2)]),
                    NP - 1: ([lambda: root_guess(4, LN2[0]), root_early()], [root_early(), root_early(last=True)])})
            nc.vector.memset(no_token, NO_TOKEN).then_inc(no_row_s, 1)
            nc.vector.tensor_copy(token.bitcast(i32), const("token"))
            dve.wait_ge(att_w_s, 16 * 8)
            dve.wait_ge(late_const_s, 16)
            add_bias(0, 0)
            normalise_batch(nc.vector, 1)
            add_bias(0, 1)
            gate_logits(0)
            dense_max(0, 0)
            dense_max(0, 1)
            for i in range(B):
                for n in range(UNITS):
                    slot_of(i, n)
            last = SEG[1][1]
            spread(11, batch(4))
            normalise(nc.vector, 1, len(SEG[0]) + len(LN2) + 5, batch(4))
            gate(B - 1)
            half_attended(B - 1)
            row_sums(batch(B - 2))
            centre(batch(B - 2))
            attended(B - 1)
            half_attended(B)
            row_sums(batch(B - 1))
            centre(batch(B - 1))

            def late_loaded(k):
                return lambda: dve.wait_ge(xid_s[k], 16)

            def root_late(last_step=False):
                return lambda: root_step(last, last_step)

            choose(1, 1, 2)
            ffn(1, {0: ([late_loaded(0)], ()),
                    1: ((), [lambda: root_guess(14, last), root_late()]),
                    2: ([root_late()], [root_late(True)]),
                    3: ([lambda: count_blocks(1, 1, 2)], [lambda: place_blocks(1, 1)]),
                    LATE[1][0] // 2: ([late_loaded(1), lambda: place_tokens(1, 1, 2)], ()),
                    CROSS[1]: ([late_loaded(2)], ())})

        @block.tensor
        def _(pe):
            def route_turn(f, g, banks):
                m = GROUPS * f + g
                if f == 0:
                    pe.wait_ge(cent_s, 1 + [RG * g < tiles.stop for tiles in LN1].index(True))
                else:
                    pe.wait_ge(cent_s, len(LN1) + len(LN2) + 1 + RG * g // 4)
                if f == 1 and RG * g == SEG[1][1].start:
                    pe.wait_ge(slot_s, 3)
                if m > 1:
                    pe.wait_ge(rt_T_s, m - (banks[0] != banks[1]))
                for k in range(RG):
                    mm = pe.transpose(bank[banks[g % 2]][:, k * 128:(k + 1) * 128], xn[:, RG * g + k, :], ident)
                mm.then_inc(rt_px_s, 1)

            def route_logits(f, g, b):
                m = GROUPS * f + g
                tiles = SEG[f][RG * g >= SEG[f][1].start]
                pe.wait_ge(rt_T_s, m + 1)
                for k in range(RG):
                    at = 512 - (tiles.stop - RG * g - k) * E
                    mm = pe.matmul(bank[b][:, at:at + E], rT[:, m % 2, k * 128:(k + 1) * 128], wr[:, :],
                                   start=True, stop=True)
                mm.then_inc(logit_s, 1)

            def rank(f, h, b):
                pe.wait_ge(hot_s, 2 * f + h + 1)
                cols = SEG_TILES[f][h] * E
                choice = hot[:, 0:SEG_TILES[f][h], :].rearrange("p t e -> p (t e)")
                pe.matmul(bank[b][:, 0:cols], const("below"), choice, start=True, stop=True)
                pe.matmul(bank[b][:, cols:2 * cols], ones[:, 0:128], choice, start=True, stop=True).then_inc(rank_s, 1)

            def turn_rows(f, j):
                pe.wait_ge(ld_s, (j + (NP * f + 1)) * 16)
                for v in range(2):
                    mm = pe.transpose(bank[5][:, v * 128:(v + 1) * 128], xs[:, v, :], ident)
                mm.then_inc(px_s, 1)

            def first_products(f, j, v, first=False):
                if v == 0 or first:
                    pe.wait_ge(xT_s, 2 * j + (2 * NP * f + v + 1))
                for k in range(KT):
                    mm = pe.matmul(bank[v][:, k * 128:(k + 1) * 128], fcb[:, v, k * 128:(k + 1) * 128], xT[:, v, :],
                                   start=True, stop=True)
                mm.then_inc(h_s, 1)

            def second_products(f, j, v):
                e = pe.value_load(expert[0:1, ds(2 * j + v, 1)], min_val=0, max_val=E - 1)
                pe.wait_ge(hT_s, 2 * j + (2 * NP * f + v + 1))
                for k in range(KT):
                    mm = pe.matmul(bank[OUT_BANK[f] + v][:, 0:128], hT[:, v, k, :], wo[:, ds(e, 1), k, :],
                                   start=(k == 0), stop=(k == KT - 1))
                mm.then_inc(py_s, 1)

            def ffn_step(f, j, first=False, last=False):
                first_products(f, j, 0)
                if first:
                    pe.wait_ge(xT_s, 2 * NP * f + 2)
                else:
                    second_products(f, j - 1, 1)
                if not last:
                    turn_rows(f, j + 1)
                first_products(f, j, 1, first)
                second_products(f, j, 0)

            def ffn(f, work):
                pe.wait_ge(ffn_w_s, 32)
                turn_rows(f, 0)
                ffn_step(f, 0, first=True)
                for lo, hi in runs(1, NP - 1, work):
                    for w in work.get(lo, ()):
                        w()
                    if hi > lo + 1:
                        with pe.Fori(lo, hi) as j:
                            ffn_step(f, j)
                    else:
                        ffn_step(f, lo)
                for w in work.get(NP - 1, ()):
                    w()
                ffn_step(f, NP - 1, last=True)
                second_products(f, NP - 1, 1)

            def turn_batch(i):
                pe.wait_ge(xb_s, i + 1)
                if i >= 3:
                    pe.wait_ge(gT_s, i - 2)
                for t in range(4):
                    mm = pe.transpose(bank[6][:, t * 128:(t + 1) * 128], xb[:, t, :], ident)
                mm.then_inc(a_px_s, 1)

            def dense_queries(i):
                pe.wait_ge(a_xT_s, i + 1)
                if i >= 3:
                    pe.wait_ge(att_s, i - 2)
                pe.matmul(bank[7][:, :], wq4[:, :], xnT[:, i % 2, :], start=True, stop=True).then_inc(q_s, 1)

            def dense_keys(i):
                pe.matmul(bank[6][:, :], wk4[:, :], xnT[:, i % 2, :], start=True, stop=True).then_inc(k_s, 1)

            def project_tiles(i, k):
                if 2 * i + k:
                    pe.wait_ge(qkg_s, 2 * i + k)
                for v in range(2):
                    t = 2 * k + v
                    mm = pe.matmul(bank[5][:, v * QKG:(v + 1) * QKG], xnT[:, i % 2, t * 128:(t + 1) * 128], wqkg[:, :],
                                   start=True, stop=True)
                mm.then_inc(qkg_p_s, 1)

            def scores(i, n):
                if n == 0:
                    pe.wait_ge(qkT_s, (DENSE + 1) * (i + 1))
                back = ahead(i, n, -2)
                if back[0] >= 0:
                    pe.wait_ge(p_s, probs_after(*back))
                t, heads = unit(n)
                s, u = bank[(n + i) % 2], i % 2
                cols = heads[-1][1] + heads[-1][2]
                a = 0 if n == 0 else DENSE * 128 + ((n - 1) % 2) * BANK_COLS[0]
                pe.matmul(s[:, 0:cols], identb[:, :], maskb[:, a:a + cols], start=True, stop=False)
                for h, a0, w in heads:
                    mm = pe.matmul(s[:, a0:a0 + w], qT[:, u, h, t * 128:(t + 1) * 128],
                                   kT[:, u, (t + 1) * 128 - w:(t + 1) * 128], start=False, stop=h == heads[-1][0])
                mm.then_inc(s_s, 1)

            def turn_probs(i, n):
                pe.wait_ge(p_s, probs_after(i, n))
                if UNITS * i + n:
                    pe.wait_ge(ptc_s, UNITS * i + n)
                for c, k in enumerate(slots(n)):
                    mm = pe.transpose(bank[3][:, c * 128:(c + 1) * 128], P[:, (n + 1) // 2 % 2, k, :], ident)
                mm.then_inc(pt_s, 1)

            def outputs(i, t):
                pe.wait_ge(ptc_s, UNITS * i + 2 * t + 1)
                if t == 0:
                    pe.wait_ge(qkg_s, 2 * i + 2)
                    if i:
                        pe.wait_ge(gated_s, i)
                u = i % 2
                v = lambda tile, h: qkg[:, u, tile, DK + h * HEAD:DK + (h + 1) * HEAD]
                o = lambda h, to: bank[4][:, (t * DENSE + h) * HEAD:(t * DENSE + to) * HEAD]
                if t:
                    pe.matmul(o(0, 1), PT[:, t % 2, 0, :], v(t - 1, 0), start=True, stop=False)
                pe.matmul(o(0, 1), PT[:, t % 2, 1, :], v(t, 0), start=(t == 0), stop=True)
                if t:
                    pe.wait_ge(v_side_s[u], 16 * (DENSE - 1) * (i // 2 + 1))
                    pe.matmul(o(1, DENSE), PT[:, t % 2, SLOTS - 1, :], v_side[:, u, t - 1, :], start=True, stop=False)
                for h in range(1, DENSE):
                    mm = pe.matmul(o(h, h + 1), PT[:, t % 2, h + 1, :], v(t, h), start=(t == 0), stop=(t == 0 or h == DENSE - 1))
                mm.then_inc(pv_s, 1)

            def turn_gated(i):
                pe.wait_ge(gated_s, i + 1)
                pe.wait_ge(qkT_s, (DENSE + 1) * min(i + 3, B))
                for t in range(4):
                    mm = pe.transpose(bank[6][:, t * 128:(t + 1) * 128], gated[:, t, :], ident)
                mm.then_inc(gp_s, 1)

            def project(i):
                pe.wait_ge(gT_s, i + 1)
                for t in range(4):
                    mm = pe.matmul(bank[7][:, t * 128:(t + 1) * 128], gT[:, t * 128:(t + 1) * 128], wproj[:, :],
                                   start=True, stop=True)
                mm.then_inc(proj_s, 1)

            def slot_of(i, n):
                nxt = ahead(i, n, 2)
                if nxt:
                    scores(*nxt)
                if n == 0 and i:
                    outputs(i - 1, 3)
                if n == 3:
                    outputs(i, 0)
                    outputs(i, 1)
                if n == 5:
                    outputs(i, 2)
                turn_probs(i, n)
                if i + 1 < B:
                    if n == 0:
                        turn_batch(i + 1)
                    if n == 1:
                        dense_queries(i + 1)
                        project_tiles(i + 1, 0)
                    if n == 2:
                        dense_keys(i + 1)
                    if n == 3:
                        project_tiles(i + 1, 1)
                if i:
                    if n == 4:
                        turn_gated(i - 1)
                    if n == 5:
                        project(i - 1)
                if i >= 2:
                    g, at = 2 * (i - 2), 5 if i + 1 == B else 1
                    if n in (at + 1, at + 2):
                        route_logits(1, g + n - at - 1, 2)
                    if n in (at, at + 1):
                        route_turn(1, g + n - at, (2, 2))
                if (i, n) == (6, 5):
                    rank(1, 0, 2)

            pe.wait_ge(const_s, 16)
            pe.wait_ge(cleared_s, 6)
            pe.wait_ge(route_w_s, 16)
            route_turn(0, 0, (6, 7))
            for g in range(GROUPS):
                if g + 1 < GROUPS:
                    route_turn(0, g + 1, (6, 7))
                route_logits(0, g, 4 if RG * g < SEG[0][0].stop else 3)
                if g == 8:
                    rank(0, 0, 4)
            rank(0, 1, 3)
            ffn(0, {})
            pe.wait_ge(att_w_s, 16 * 8)
            pe.wait_ge(masks_s, 2)
            turn_batch(0)
            dense_queries(0)
            dense_keys(0)
            for k in range(2):
                project_tiles(0, k)
            scores(0, 0)
            scores(0, 1)
            pe.wait_ge(y_s, 2 * NP)
            for i in range(B):
                for n in range(UNITS):
                    slot_of(i, n)

            route_logits(1, 11, 2)
            outputs(B - 1, 3)
            turn_gated(B - 1)
            project(B - 1)

            def last_added():
                pe.wait_ge(att_s, B)

            for pair in ((12, 13), (14, 15)):
                for g in pair:
                    route_turn(1, g, (2, 4))
                for g in pair:
                    route_logits(1, g, 2)
            last_added()
            ffn(1, {1: [lambda: rank(1, 1, 2)]})


def kernel(**inputs):
    import numpy as np
    import concourse.bacc as bacc
    from concourse import mybir as mb
    from concourse.bass_utils import run_bass_kernel_spmd as run

    a = {k.split("_", 1)[1]: np.ascontiguousarray(v) for k, v in inputs.items()}
    wqk, bqk = a["attn_Wqk"], a["attn_bqk"]

    def spread_heads(w):
        z = np.zeros((w.shape[0], 32 - HEAD), w.dtype)
        return np.concatenate([p for h in range(DENSE) for p in (w[:, h * HEAD:(h + 1) * HEAD], z)], axis=1)

    p = np.arange(128)
    key = np.arange(-128, 128)
    lag = p[:, None] - key[None, :]
    off = [np.where((lag >= 0) & (lag < w), 0.0, -BIG) for w in WINDOWS[:DENSE]]
    o = np.arange(7, -1, -1)
    light = np.where(p[:, None, None] < o[None, :, None], -BIG, np.zeros((128, 8, LIGHT)))
    consts = {
        "ident": np.eye(128), "below": np.triu(np.ones((128, 128)), 1),
        "mask_first": np.concatenate([m[:, 128:] for m in off], axis=1),
        "mask_rest": np.concatenate([m[:, 128 - v:] for m, v in zip(off, PREV)], axis=1),
        "light_mask": light.reshape(128, -1),
        "first_of_ties": np.tile(np.arange(E, 0, -1), (128, 1)),
        "block_no": np.tile(np.arange(max(max(n) for n in NBS)), (128, 1)),
        "full_blocks": np.tile(128 * np.arange(MOST), (128, 1)),
        "token": p[:, None] + 128 * np.arange(N_TILES)[None, :],
        "head_scale": SCALE * (p[:, None] // 32 == np.arange(DENSE)[None, :]),
    }
    consts = np.concatenate([consts[n] for n in CONST], axis=1).astype(np.float32)
    no_bias = np.zeros(HEAD, bqk.dtype)
    b_q4 = np.concatenate([spread_heads(np.concatenate([bqk[h * HEAD:(h + 1) * HEAD] if g == h else no_bias
                                                        for g in range(DENSE)])[None, :]).reshape(128, 1)
                           for h in range(DENSE)], axis=1)
    arrays = {
        "x": a["attn_x"],
        "w_qkg": np.concatenate([wqk[:, DENSE * HEAD:], a["attn_Wgate"]], axis=1),
        "b_qkg": np.concatenate([bqk[DENSE * HEAD:], a["attn_bgate"]])[None, :],
        "w_q4": spread_heads(wqk[:, :C]), "w_k4": spread_heads(wqk[:, C:]),
        "b_q4": b_q4, "b_k4": spread_heads(bqk[None, C:]).reshape(128, 1),
        "w_proj": a["attn_Wproj"], "b_proj": a["attn_bproj"][None, :],
        "w_router": a["ffn_router_w"].T, "w_fc": a["ffn_expert_fc"],
        "w_out": a["ffn_expert_proj"].transpose(0, 2, 1), "consts": consts,
    }
    arrays = {k: np.ascontiguousarray(v) for k, v in arrays.items()}
    nc = bacc.Bacc("TRN2", target_bir_lowering=False, num_devices=1)
    args = [nc.dram_tensor(f"in_{n}", v.shape, mb.dt.from_np(v.dtype), kind="ExternalInput").ap() for n, v in arrays.items()]
    out = nc.dram_tensor("out_rows", (B, T, C), mb.dt.float32, kind="ExternalOutput").ap()
    macaron(nc, *args, out)
    r = run(nc, [{f"in_{n}": v for n, v in arrays.items()}], core_ids=[0])
    return r.results[0]["out_rows"]
```
